# Optimizing a Trainium2 kernel written in Bass

```python
import numpy as np
import jax
import jax.numpy as jnp

def _softmax(x, axis=-1):
    return jax.nn.softmax(x, axis=axis)

def _gelu(x):
    return jax.nn.gelu(x, approximate=True)

def _silu(x):
    return jax.nn.silu(x)

def _sigmoid(x):
    return jax.nn.sigmoid(x)

def _layernorm(x, axis=-1, eps=1e-05):
    m = jnp.mean(x, axis=axis, keepdims=True)
    v = jnp.var(x, axis=axis, keepdims=True)
    return (x - m) / jnp.sqrt(v + eps)

def _scatter_add(tgt, idx, src, axis=0):
    return tgt.at[idx].add(src)

def _segment_sum(src, seg, n):
    return jax.ops.segment_sum(src, seg, n)
kernel_name = 'mk_decoder_postln_d1_seqx_r8_bbb824'

def setup_inputs(seed: int=0):
    np.random.seed(seed)
    _w = jnp.asarray

    def _rec_inputs():
        import jax
        import jax.numpy as jnp
        _rk = jax.random.key(seed)
        x = -0.0005207 + 1.001 * jax.random.normal(jax.random.fold_in(_rk, 1), (64, 64, 128), jnp.float32)
        _lenS = 64 - jax.random.randint(jax.random.fold_in(_rk, 7), (64,), 0, max(1, 64 // 4) + 1, jnp.int32)
        _lenS2 = 64 - jax.random.randint(jax.random.fold_in(_rk, 8), (64,), 0, max(1, 64 // 4) + 1, jnp.int32)
        _ctx_1024P = jax.random.normal(jax.random.fold_in(_rk, 11), (64, 16, 128), jnp.float32)
        _ctx_1024c = jax.random.dirichlet(jax.random.fold_in(_rk, 511), 0.3 * jnp.ones((16,), jnp.float32), (64, 64))
        _ctx_1024t = jnp.einsum('bsk,bkd->bsd', _ctx_1024c, _ctx_1024P)
        _ctx_1024t = _ctx_1024t * jax.lax.rsqrt(jnp.mean(jnp.square(_ctx_1024t)) + 1e-12) * 0.953939
        ctx_1024 = -0.000514642 + 1.00011 * (_ctx_1024t + 0.3 * jax.random.normal(jax.random.fold_in(_rk, 611), (64, 64, 128), jnp.float32))
        return (x, ctx_1024)
    x, ctx_1024 = _rec_inputs()

    def _L0_attn_setup():
        import jax, jax.numpy as jnp
        import numpy as np
        DIM_EMB = 128
        NUM_HEADS = 16
        DIM_HEAD = DIM_EMB // NUM_HEADS
        key = jax.random.key(seed)
        k1, k2, k3 = jax.random.split(key, 3)
        x = jax.random.normal(k1, (4, 256, DIM_EMB), dtype=jnp.float32)
        w_qkv = jax.random.normal(k2, (3 * NUM_HEADS * DIM_HEAD, DIM_EMB), dtype=jnp.float32) * DIM_EMB ** (-0.5)
        w_out = jax.random.normal(k3, (DIM_EMB, NUM_HEADS * DIM_HEAD), dtype=jnp.float32) * (NUM_HEADS * DIM_HEAD) ** (-0.5)
        return {'x': x, 'w_qkv': w_qkv, 'w_out': w_out}
    _L0_attn_all = _L0_attn_setup()
    _L0_attn_in = {k: v for k, v in _L0_attn_all.items() if k in ('w_qkv', 'w_out')}
    del _L0_attn_all

    def _L0_xattn_setup():
        import jax, jax.numpy as jnp
        import numpy as np
        EMBED_DIM = 128
        NUM_HEADS = 16
        HEAD_DIM = EMBED_DIM // NUM_HEADS
        WINDOW = 64

        def apply_rope(x):
            B, H, S, d = x.shape
            half = d // 2
            pos = jnp.arange(S, dtype=x.dtype)
            freqs = 1.0 / 10000.0 ** (jnp.arange(half, dtype=x.dtype) / half)
            ang = pos[:, None] * freqs[None, :]
            cos, sin = (jnp.cos(ang), jnp.sin(ang))
            x1, x2 = (x[..., :half], x[..., half:])
            return jnp.concatenate([x1 * cos - x2 * sin, x1 * sin + x2 * cos], axis=-1)

        def _forward(query, key, value, q_w, q_b, k_w, k_b, v_w, v_b, o_w, o_b):
            B, S_q, D = query.shape
            S_k = key.shape[1]
            H, d, W = (NUM_HEADS, HEAD_DIM, WINDOW)
            q = (query @ q_w.T + q_b).reshape(B, S_q, H, d).transpose(0, 2, 1, 3)
            k = (key @ k_w.T + k_b).reshape(B, S_k, H, d).transpose(0, 2, 1, 3)
            v = (value @ v_w.T + v_b).reshape(B, S_k, H, d).transpose(0, 2, 1, 3)
            q = apply_rope(q) * d ** (-0.5)
            k = apply_rope(k)
            q_pos = jnp.arange(S_q)[:, None]
            offsets = jnp.arange(-W, 1)[None, :]
            idx = q_pos + offsets
            local_mask = (idx < 0) | (idx >= S_k)
            gidx = jnp.clip(idx, 0, S_k - 1)
            k_win = k[:, :, gidx, :]
            v_win = v[:, :, gidx, :]
            scores = jnp.einsum('bhqd,bhqwd->bhqw', q, k_win)
            mask = local_mask[None, None, :, :]
            scores = jnp.where(mask, -jnp.inf, scores)
            m = jnp.max(scores, axis=-1, keepdims=True)
            m = jnp.where(jnp.isfinite(m), m, 0.0)
            e = jnp.exp(scores - m)
            denom = jnp.sum(e, axis=-1, keepdims=True)
            probs = jnp.where(denom > 0, e / jnp.where(denom > 0, denom, 1.0), 0.0)
            ctx = jnp.einsum('bhqw,bhqwd->bhqd', probs, v_win)
            ctx = ctx.transpose(0, 2, 1, 3).reshape(B, S_q, D)
            return ctx @ o_w.T + o_b
        key = jax.random.key(seed)
        ks = jax.random.split(key, 12)
        B, S, D = (1, 256, EMBED_DIM)
        scale = 1.0 / np.sqrt(D)
        inp = {'query': jax.random.normal(ks[0], (B, S, D), jnp.float32), 'key': jax.random.normal(ks[1], (B, S, D), jnp.float32), 'value': jax.random.normal(ks[2], (B, S, D), jnp.float32), 'q_w': jax.random.normal(ks[3], (D, D), jnp.float32) * scale, 'q_b': jax.random.normal(ks[4], (D,), jnp.float32) * 0.01, 'k_w': jax.random.normal(ks[5], (D, D), jnp.float32) * scale, 'k_b': jax.random.normal(ks[6], (D,), jnp.float32) * 0.01, 'v_w': jax.random.normal(ks[7], (D, D), jnp.float32) * scale, 'v_b': jax.random.normal(ks[8], (D,), jnp.float32) * 0.01, 'o_w': jax.random.normal(ks[9], (D, D), jnp.float32) * scale, 'o_b': jax.random.normal(ks[10], (D,), jnp.float32) * 0.01}
        return inp
    _L0_xattn_all = _L0_xattn_setup()
    _L0_xattn_in = {k: v for k, v in _L0_xattn_all.items() if k in ('q_w', 'q_b', 'k_w', 'k_b', 'v_w', 'v_b', 'o_w', 'o_b')}
    del _L0_xattn_all

    def _L0_ffn_setup():
        import jax, jax.numpy as jnp
        import numpy as np
        D = 128
        F = 128
        E = 8
        K = 2
        B, T = (2, 256)

        def _moe_forward(x, router_w, w1, w2, shared_gate_up, shared_down, shared_gate_w):
            b, t, d = x.shape
            xf = x.reshape(-1, d)
            n = xf.shape[0]
            logits = xf @ router_w
            probs = jax.nn.softmax(logits, axis=-1)
            topw, topi = jax.lax.top_k(probs, K)
            combine = jnp.zeros((n, E), dtype=probs.dtype).at[jnp.arange(n)[:, None], topi].add(topw)
            h = jax.nn.silu(jnp.einsum('nd,edf->nef', xf, w1))
            ye = jnp.einsum('nef,efd->ned', h, w2)
            routed = jnp.einsum('ne,ned->nd', combine, ye)
            gu = xf @ shared_gate_up
            gate, up = (gu[:, :F], gu[:, F:])
            shared = jax.nn.silu(gate) * up @ shared_down
            shared = jax.nn.sigmoid(xf @ shared_gate_w) * shared
            return (routed + shared).reshape(b, t, d)
        key = jax.random.key(seed)
        ks = jax.random.split(key, 7)
        std = 0.02
        x = jax.random.normal(ks[0], (B, T, D), dtype=jnp.float32)
        router_w = jax.random.normal(ks[1], (D, E), dtype=jnp.float32) * std
        w1 = jax.random.normal(ks[2], (E, D, F), dtype=jnp.float32) * std
        w2 = jax.random.normal(ks[3], (E, F, D), dtype=jnp.float32) * std
        shared_gate_up = jax.random.normal(ks[4], (D, 2 * F), dtype=jnp.float32) * std
        shared_down = jax.random.normal(ks[5], (F, D), dtype=jnp.float32) * std
        shared_gate_w = jax.random.normal(ks[6], (D, 1), dtype=jnp.float32) * std
        return {'x': x, 'router_w': router_w, 'w1': w1, 'w2': w2, 'shared_gate_up': shared_gate_up, 'shared_down': shared_down, 'shared_gate_w': shared_gate_w}
    _L0_ffn_all = _L0_ffn_setup()
    _L0_ffn_in = {k: v for k, v in _L0_ffn_all.items() if k in ('router_w', 'w1', 'w2', 'shared_gate_up', 'shared_down', 'shared_gate_w')}
    del _L0_ffn_all
    return {'x': x, 'ctx_1024': ctx_1024, 'L0_attn_w_qkv': _L0_attn_in['w_qkv'], 'L0_attn_w_out': _L0_attn_in['w_out'], 'L0_xattn_q_w': _L0_xattn_in['q_w'], 'L0_xattn_q_b': _L0_xattn_in['q_b'], 'L0_xattn_k_w': _L0_xattn_in['k_w'], 'L0_xattn_k_b': _L0_xattn_in['k_b'], 'L0_xattn_v_w': _L0_xattn_in['v_w'], 'L0_xattn_v_b': _L0_xattn_in['v_b'], 'L0_xattn_o_w': _L0_xattn_in['o_w'], 'L0_xattn_o_b': _L0_xattn_in['o_b'], 'L0_ffn_router_w': _L0_ffn_in['router_w'], 'L0_ffn_w1': _L0_ffn_in['w1'], 'L0_ffn_w2': _L0_ffn_in['w2'], 'L0_ffn_shared_gate_up': _L0_ffn_in['shared_gate_up'], 'L0_ffn_shared_down': _L0_ffn_in['shared_down'], 'L0_ffn_shared_gate_w': _L0_ffn_in['shared_gate_w']}

def reference(x, ctx_1024, L0_attn_w_qkv, L0_attn_w_out, L0_xattn_q_w, L0_xattn_q_b, L0_xattn_k_w, L0_xattn_k_b, L0_xattn_v_w, L0_xattn_v_b, L0_xattn_o_w, L0_xattn_o_b, L0_ffn_router_w, L0_ffn_w1, L0_ffn_w2, L0_ffn_shared_gate_up, L0_ffn_shared_down, L0_ffn_shared_gate_w):
    import jax
    import jax.numpy as jnp

    def _L0_attn_ref(x, w_qkv, w_out):
        import jax, jax.numpy as jnp
        import numpy as np
        DIM_EMB = 128
        NUM_HEADS = 16
        DIM_HEAD = DIM_EMB // NUM_HEADS
        b, t, _ = x.shape
        scale = DIM_HEAD ** (-0.5)
        qkv = jnp.einsum('bte,fe->btf', x, w_qkv)
        qkv = qkv.reshape(b, t, 3, NUM_HEADS, DIM_HEAD)
        q, k, v = (qkv[:, :, 0], qkv[:, :, 1], qkv[:, :, 2])
        scores = jnp.einsum('bihd,bjhd->bhij', q, k) * scale
        weights = jax.nn.softmax(scores, axis=-1)
        attn = jnp.einsum('bhij,bjhd->bhid', weights, v)
        concat = attn.transpose(0, 2, 1, 3).reshape(b, t, NUM_HEADS * DIM_HEAD)
        return jnp.einsum('btf,ef->bte', concat, w_out)

    def _L0_xattn_ref(query, key, value, q_w, q_b, k_w, k_b, v_w, v_b, o_w, o_b):
        import jax, jax.numpy as jnp
        import numpy as np
        EMBED_DIM = 128
        NUM_HEADS = 16
        HEAD_DIM = EMBED_DIM // NUM_HEADS
        WINDOW = 64

        def apply_rope(x):
            B, H, S, d = x.shape
            half = d // 2
            pos = jnp.arange(S, dtype=x.dtype)
            freqs = 1.0 / 10000.0 ** (jnp.arange(half, dtype=x.dtype) / half)
            ang = pos[:, None] * freqs[None, :]
            cos, sin = (jnp.cos(ang), jnp.sin(ang))
            x1, x2 = (x[..., :half], x[..., half:])
            return jnp.concatenate([x1 * cos - x2 * sin, x1 * sin + x2 * cos], axis=-1)

        def _forward(query, key, value, q_w, q_b, k_w, k_b, v_w, v_b, o_w, o_b):
            B, S_q, D = query.shape
            S_k = key.shape[1]
            H, d, W = (NUM_HEADS, HEAD_DIM, WINDOW)
            q = (query @ q_w.T + q_b).reshape(B, S_q, H, d).transpose(0, 2, 1, 3)
            k = (key @ k_w.T + k_b).reshape(B, S_k, H, d).transpose(0, 2, 1, 3)
            v = (value @ v_w.T + v_b).reshape(B, S_k, H, d).transpose(0, 2, 1, 3)
            q = apply_rope(q) * d ** (-0.5)
            k = apply_rope(k)
            q_pos = jnp.arange(S_q)[:, None]
            offsets = jnp.arange(-W, 1)[None, :]
            idx = q_pos + offsets
            local_mask = (idx < 0) | (idx >= S_k)
            gidx = jnp.clip(idx, 0, S_k - 1)
            k_win = k[:, :, gidx, :]
            v_win = v[:, :, gidx, :]
            scores = jnp.einsum('bhqd,bhqwd->bhqw', q, k_win)
            mask = local_mask[None, None, :, :]
            scores = jnp.where(mask, -jnp.inf, scores)
            m = jnp.max(scores, axis=-1, keepdims=True)
            m = jnp.where(jnp.isfinite(m), m, 0.0)
            e = jnp.exp(scores - m)
            denom = jnp.sum(e, axis=-1, keepdims=True)
            probs = jnp.where(denom > 0, e / jnp.where(denom > 0, denom, 1.0), 0.0)
            ctx = jnp.einsum('bhqw,bhqwd->bhqd', probs, v_win)
            ctx = ctx.transpose(0, 2, 1, 3).reshape(B, S_q, D)
            return ctx @ o_w.T + o_b
        return _forward(query, key, value, q_w, q_b, k_w, k_b, v_w, v_b, o_w, o_b)

    def _L0_ffn_ref(x, router_w, w1, w2, shared_gate_up, shared_down, shared_gate_w):
        import jax, jax.numpy as jnp
        import numpy as np
        D = 128
        F = 128
        E = 8
        K = 2
        B, T = (2, 256)

        def _moe_forward(x, router_w, w1, w2, shared_gate_up, shared_down, shared_gate_w):
            b, t, d = x.shape
            xf = x.reshape(-1, d)
            n = xf.shape[0]
            logits = xf @ router_w
            probs = jax.nn.softmax(logits, axis=-1)
            topw, topi = jax.lax.top_k(probs, K)
            combine = jnp.zeros((n, E), dtype=probs.dtype).at[jnp.arange(n)[:, None], topi].add(topw)
            h = jax.nn.silu(jnp.einsum('nd,edf->nef', xf, w1))
            ye = jnp.einsum('nef,efd->ned', h, w2)
            routed = jnp.einsum('ne,ned->nd', combine, ye)
            gu = xf @ shared_gate_up
            gate, up = (gu[:, :F], gu[:, F:])
            shared = jax.nn.silu(gate) * up @ shared_down
            shared = jax.nn.sigmoid(xf @ shared_gate_w) * shared
            return (routed + shared).reshape(b, t, d)
        return _moe_forward(x, router_w, w1, w2, shared_gate_up, shared_down, shared_gate_w)
    x = _layernorm(x + _L0_attn_ref(x, L0_attn_w_qkv, L0_attn_w_out), axis=-1)
    x = _layernorm(x + _L0_xattn_ref(x, ctx_1024, ctx_1024, L0_xattn_q_w, L0_xattn_q_b, L0_xattn_k_w, L0_xattn_k_b, L0_xattn_v_w, L0_xattn_v_b, L0_xattn_o_w, L0_xattn_o_b), axis=-1)
    x = _layernorm(x + _L0_ffn_ref(x, L0_ffn_router_w, L0_ffn_w1, L0_ffn_w2, L0_ffn_shared_gate_up, L0_ffn_shared_down, L0_ffn_shared_gate_w), axis=-1)
    return x

_drawn_inputs = setup_inputs


def setup_inputs(seed=0):
    import zlib

    import numpy as np

    out = dict(_drawn_inputs(seed))
    spreads = {}
    factors = {'L0_xattn_q_b': 8.0,
     'L0_xattn_k_b': 8.0,
     'L0_xattn_v_b': 5.803,
     'L0_xattn_o_b': 5.819,
     'L0_ffn_router_w': 8.0,
     'L0_ffn_w1': 8.0,
     'L0_ffn_w2': 8.0,
     'L0_ffn_shared_gate_up': 8.0,
     'L0_ffn_shared_down': 8.0,
     'L0_ffn_shared_gate_w': 8.0}
    for name, (base, spread) in spreads.items():
        noise = np.random.default_rng([zlib.crc32(name.encode()), seed]).standard_normal(out[name].shape)
        drawn = base * np.exp(spread * noise) if base else spread * noise
        out[name] = jnp.asarray(drawn.astype(out[name].dtype))
    for name, factor in factors.items():
        out[name] = (out[name] * factor).astype(out[name].dtype)
    return out
```

```python
from contextlib import ExitStack

import numpy as np

import concourse.bass as bass
from concourse import mybir

ALU = mybir.AluOpType
ACT = mybir.ActivationFunctionType
F32 = mybir.dt.float32
F16 = mybir.dt.float16
BF16 = mybir.dt.bfloat16
AX_X = mybir.AxisListType.X

P = 128
D = 128
H, DH, S = 16, 8, 64
TOKENS = 64 * S
TILES = 4
G = TILES * P
NG = TOKENS // G
E = 8
PAIRS = H // 2
BANKS = 8
MASKED = -1.0e30
EPS = 1e-5
SCALE = float(DH) ** -0.5

W_QA, W_KA, W_VA, W_QB, W_QBR, W_KB, W_KBR, W_VB = range(8)
W_1 = 8
W_GATE, W_UP = W_1 + E, W_1 + E + 1
W_2 = W_UP + 1
W_DOWN = W_2 + E
W_OA = W_DOWN + 1
W_OB = W_OA + 8
NW = W_OB + 8

ROUTER = 16
STACK = 16 * 15
N_LOADS = 12
ZERO_FILLS = 5


def decoder_layer(nc, x, x_t, ctx_t, weights, router, row_consts, biases, c_ident, c_ident16, c_masks,
                  c_den_ones, c_spread, c_pick, out):
    ctx = ExitStack()
    with ctx:
        def sb(name, shape, dt=F32):
            return ctx.enter_context(nc.sbuf_tensor(name, shape, dt))

        def sem(name):
            return ctx.enter_context(nc.semaphore(name))

        w = sb("w", [P, NW, D])
        rw = sb("rw", [P, E + 1])
        rows3 = sb("rows3", [P, 3, D])
        bias = sb("bias", [P, 4])
        ident = sb("ident", [P, P])
        ident16 = sb("ident16", [P, P], BF16)
        masks = sb("masks", [P, 3, S], BF16)
        den_ones = sb("den_ones", [P, 8, 32])
        spread = sb("spread", [P, 8, P])
        pick = sb("pick", [P, E + 1, P], BF16)
        half_neg = sb("half_neg", [P, TILES])
        seg = sb("seg", [P, TILES, E])
        xt = sb("xt", [P, G])
        ct = sb("ct", [P, G])
        xn = sb("xn", [P, TILES, D])
        split = {n: sb("split_" + n, [P, 2, G], F16) for n in ("qA", "kA", "qB", "kB")}
        q_rows = {a: sb("q_rows" + a, [P, 4, G], F16) for a in "AB"}
        k_rows = {a: sb("k_rows" + a, [P, 4, G], F16) for a in "AB"}
        q_block = {a: sb("q_block" + a, [P, 4, 4, G], F16) for a in "AB"}
        k_block = {a: sb("k_block" + a, [P, 4, 4, G], F16) for a in "AB"}
        v_block = {a: sb("v_block" + a, [P, TILES, PAIRS, 32]) for a in "AB"}
        neg_max = {a: sb("neg_max" + a, [P, TILES, H]) for a in "AB"}
        neg_max_t = {a: sb("neg_max_t" + a, [H, G], F16) for a in "AB"}
        probs = sb("probs", [P, 2, H * S])
        ctx_raw = sb("ctx_raw", [P, TILES, 256])
        inv_den = sb("inv_den", [P, P])
        ctx_n = sb("ctx_n", [P, TILES, 256])
        roped = sb("roped", [P, 2, G])
        rope_sum = sb("rope_sum", [P, G])
        res = sb("res", [P, TILES, D])
        stats = sb("stats", [P, TILES, 6])
        mean_var = sb("mean_var", [P, TILES, 2])
        rstd = sb("rstd", [P, TILES])
        veps = sb("veps", [P, TILES])
        eps = sb("eps", [P, TILES])
        x1 = sb("x1", [P, TILES, D])
        x1b = sb("x1b", [P, TILES, D])
        x1t = sb("x1t", [P, G])
        x2 = sb("x2", [P, TILES, D])
        x2t = sb("x2t", [P, G])
        x3 = sb("x3", [P, TILES, D])
        logit = sb("logit", [P, TILES, E + 1])
        top = sb("top", [P, TILES, 8])
        small = [sb(f"small{k}", [P, TILES, E]) for k in range(6)]
        col = [sb(f"col{k}", [P, TILES]) for k in range(4)]
        gate = sb("gate", [P, TILES, E + 1])
        gate_r = sb("gate_r", [P, 2, TILES, E + 1])
        gate3 = sb("gate3", [P, TILES, 96], BF16)
        gate_t = sb("gate_t", [P, G], BF16)
        act_h = sb("act_h", [P, 2, G])
        sh_h = sb("sh_h", [P, G])
        gated = sb("gated", [P, 2, G])
        yt = sb("yt", [P, G])

        bank = [ctx.enter_context(nc.psum_tensor(f"bank{i}", [P, 512], F32)) for i in range(BANKS)]
        scratch = {a: nc.dram_tensor("split_" + a, [4, P, G], F16).ap() for a in "AB"}

        score_bank, t_bank = bank[0:2], bank[2:4]
        ctx_bank, y_bank, den_bank, side_bank = bank[4], bank[5], bank[6], bank[7]

        def per_attention(name):
            return {a: sem(name + a) for a in "AB"}

        loaded, pool_const, rows_zero = sem("weights_loaded"), sem("pool_const"), sem("rows_zero")
        zeroed = per_attention("zeroed")
        carried = sem("waits_carried")
        xt_in, ct_in, xn_in, stored = sem("xt_in"), sem("ct_in"), sem("xn_in"), sem("stored")
        q_written, k_written = per_attention("q_written"), per_attention("k_written")
        v_written, v_placed = per_attention("v_written"), per_attention("v_placed")
        hi_ready, split_ready = per_attention("hi_ready"), per_attention("split_ready")
        spilled = per_attention("spilled")
        q_stacked, k_stacked = per_attention("q_stacked"), per_attention("k_stacked")
        roped_ready, rope_sum_ready = sem("roped_ready"), sem("rope_sum_ready")
        scores_written, max_ready = per_attention("scores_written"), per_attention("max_ready")
        max_turned, max_t_ready = per_attention("max_turned"), per_attention("max_t_ready")
        max_stacked = per_attention("max_stacked")
        t_written, probs_ready = per_attention("t_written"), per_attention("probs_ready")
        probs_used = per_attention("probs_used")
        ctx_written, ctx_kept = per_attention("ctx_written"), per_attention("ctx_kept")
        inv_ready = per_attention("inv_ready")
        spread_written, ctx_n_ready = per_attention("spread_written"), per_attention("ctx_n_ready")
        y_written, x_turned, xt_ready = (per_attention("y_written"), per_attention("x_turned"),
                                         per_attention("xt_ready"))
        norms = "ABC"
        res_ready, rstd_ready, normed = ({a: sem(name + a) for a in norms}
                                         for name in ("res_ready", "rstd_ready", "normed"))
        stats_ready, var_ready = ({a: sem(name + a) for a in norms} for name in ("stats_ready", "var_ready"))
        veps_ready = {a: sem("veps_ready" + a) for a in norms}
        biased = sem("biased")
        logits_written, logit_ready, exp_ready = sem("logits_written"), sem("logit_ready"), sem("exp_ready")
        router_step, gate_step = sem("router_step"), sem("gate_step")
        gate_turned, gate_t_ready = sem("gate_turned"), sem("gate_t_ready")
        h_written, silu_ready, gates_written = sem("h_written"), sem("silu_ready"), sem("gates_written")
        up_written, sh_ready = sem("up_written"), sem("sh_ready")
        x3_free = sem("x3_free")
        gated_ready, gated_used = sem("gated_ready"), sem("gated_used")
        sum_written, yt_ready, out_turned = sem("sum_written"), sem("yt_ready"), sem("out_turned")

        block = ctx.enter_context(nc.Block())

        def steps(step, eng):
            step(0, a=True, b=False, nxt=True)
            with eng.Fori(1, NG - 1) as n:
                step(n, a=True, b=True, nxt=True)
            step(NG - 1, a=True, b=True, nxt=False)
            step(NG, a=False, b=True, nxt=False)

        @block.sync
        def _(sp):
            sp.dma_start(xt[:], x_t[0]).then_inc(xt_in, 16)
            sp.dma_start(w[:, 0:W_1], weights[:, 0:W_1]).then_inc(loaded, 16)
            for dst, src in ((rw, router), (rows3, row_consts), (bias, biases), (ident, c_ident),
                             (ident16, c_ident16), (masks, c_masks), (den_ones, c_den_ones),
                             (spread, c_spread), (pick, c_pick)):
                sp.dma_start(dst[:], src).then_inc(loaded, 16)
            sp.dma_start(ct[:], ctx_t[0]).then_inc(ct_in, 16)
            sp.dma_start(xn[:], x[0]).then_inc(xn_in, 16)
            sp.dma_start(w[:, W_OA:NW], weights[:, W_OA:NW]).then_inc(loaded, 16)
            sp.dma_start(w[:, W_1:W_OA], weights[:, W_1:W_OA]).then_inc(loaded, 16)

            def carry(n):
                if not isinstance(n, int):
                    sp.sem_inc(carried, 1)

            def stack(a, part):
                base = 0 if part == "q" else 2
                order = (0, 0, 1) if part == "q" else (0, 1, 0)
                rows, blocks = (q_rows, q_block) if part == "q" else (k_rows, k_block)
                done = (q_stacked if part == "q" else k_stacked)[a]
                for s, hl in enumerate(order):
                    src = scratch[a][base + hl].rearrange("(g r) t -> r g t", g=4)
                    sp.dma_start(rows[a][32 * s:32 * s + 32], src).then_inc(done, 16)
                    for r in range(4):
                        sp.dma_start(blocks[a][32 * s + 8 * r:32 * s + 8 * r + 8, :, r, :],
                                     src[8 * r:8 * r + 8]).then_inc(done, 16)

            def spill(a, part):
                base = 0 if part == "q" else 2
                sp.dma_start(scratch[a][base:base + 2].rearrange("s p t -> p s t"),
                             split[part + a][:]).then_inc(spilled[a], 16)

            def maxima(a):
                for r in range(4):
                    sp.dma_start(q_block[a][96 + r:97 + r, :, r, :],
                                 neg_max_t[a][4 * r:4 * r + 4]).then_inc(max_stacked[a], 16)

            def step(n, a, b, nxt):
                m = n - 1
                if nxt:
                    sp.wait_ge(v_written["A"], n + 1)
                    carry(n)
                    sp.dma_start(xt[:], x_t[n + 1]).then_inc(xt_in, 16)
                    sp.wait_ge(q_stacked["A"], STACK * n + STACK)
                    carry(n)
                    sp.wait_ge(split_ready["A"], 2 * n + 3)
                    carry(n)
                    spill("A", "q")
                    sp.wait_ge(k_stacked["A"], STACK * n + STACK)
                    carry(n)
                    sp.wait_ge(split_ready["A"], 2 * n + 4)
                    carry(n)
                    spill("A", "k")
                if a:
                    sp.wait_ge(max_t_ready["A"], n + 1)
                    carry(n)
                    maxima("A")
                if b:
                    sp.wait_ge(max_t_ready["B"], m + 1)
                    carry(n)
                    maxima("B")
                if nxt:
                    sp.wait_ge(spilled["A"], 32 * n + 64)
                    carry(n)
                    sp.wait_ge(t_written["A"], 8 * n + 8)
                    carry(n)
                    stack("A", "q")
                    stack("A", "k")
                if a:
                    sp.wait_ge(split_ready["B"], 2 * n + 1)
                    carry(n)
                    if b:
                        sp.wait_ge(k_stacked["B"], STACK * n)
                        carry(n)
                    spill("B", "k")
                    sp.wait_ge(spilled["B"], 32 * n + 16)
                    carry(n)
                    if b:
                        sp.wait_ge(t_written["B"], 8 * m + 8)
                        carry(n)
                    stack("B", "k")
                if nxt:
                    sp.wait_ge(res_ready["A"], n + 1)
                    carry(n)
                    sp.dma_start(xn[:], x[n + 1]).then_inc(xn_in, 16)
                    sp.wait_ge(v_written["B"], n + 1)
                    carry(n)
                    sp.dma_start(ct[:], ctx_t[n + 1]).then_inc(ct_in, 16)
                if a:
                    sp.wait_ge(split_ready["B"], 2 * n + 2)
                    carry(n)
                    if b:
                        sp.wait_ge(q_stacked["B"], STACK * n)
                        carry(n)
                    spill("B", "q")
                    sp.wait_ge(spilled["B"], 32 * n + 32)
                    carry(n)
                    stack("B", "q")

            sp.wait_ge(zeroed["A"], ZERO_FILLS)
            sp.wait_ge(zeroed["B"], ZERO_FILLS)
            sp.wait_ge(split_ready["A"], 1)
            spill("A", "q")
            sp.wait_ge(split_ready["A"], 2)
            spill("A", "k")
            sp.wait_ge(spilled["A"], 32)
            stack("A", "q")
            stack("A", "k")
            steps(step, sp)

        @block.gpsimd
        def _(pool):
            for a in "AB":
                pool.memset(q_block[a][:], 0.0).then_inc(zeroed[a], 1)
            pool.memset(half_neg[:], -0.5).then_inc(pool_const, 1)
            pool.memset(eps[:], EPS).then_inc(pool_const, 1)
            pool.memset(gate3[:], 0.0).then_inc(pool_const, 1)
            pool.memset(seg[:], 1.0).then_inc(pool_const, 1)
            pool.wait_ge(pool_const, 4)
            pool.memset(seg[:, :, 0:1], 0.0).then_inc(pool_const, 1)
            pool.wait_ge(loaded, 16 * N_LOADS)
            pool.sem_inc(x3_free, 1)

            def rope_sum_and_lo(n, part, k):
                pool.wait_ge(roped_ready, 4 * n + 2 * k)
                pool.tensor_tensor(rope_sum[:], roped[:, 0, :], roped[:, 1, :], ALU.add)\
                    .then_inc(rope_sum_ready, 1)
                pool.wait_ge(rope_sum_ready, 2 * n + k)
                pool.wait_ge(hi_ready["B"], 2 * n + k)
                pool.tensor_tensor(split[part + "B"][:, 1, :], rope_sum[:], split[part + "B"][:, 0, :],
                                   ALU.subtract).then_inc(split_ready["B"], 1)

            def inverse_root(n, j):
                pool.wait_ge(var_ready[j], 4 * n + 4)
                pool.tensor_tensor(veps[:], mean_var[:, :, 1], eps[:], ALU.add).then_inc(veps_ready[j], 1)
                pool.wait_ge(veps_ready[j], n + 1)
                pool.tensor_tensor(rstd[:], veps[:], half_neg[:], ALU.pow).then_inc(rstd_ready[j], 1)

            def bias_residual(n):
                pool.wait_ge(normed["A"], n + 1)
                pool.tensor_tensor(x1b[:], x1[:], rows3[:, 1:2, :].to_broadcast([P, TILES, D]), ALU.add)\
                    .then_inc(biased, 1)

            def step(n, a, b, nxt):
                m = n - 1
                if a:
                    rope_sum_and_lo(n, "k", 1)
                    inverse_root(n, "A")
                if b:
                    inverse_root(m, "B")
                    pool.wait_ge(res_ready["B"], m + 1)
                if a:
                    bias_residual(n)
                    rope_sum_and_lo(n, "q", 2)
                if b:
                    inverse_root(m, "C")
                    pool.wait_ge(normed["C"], m + 1)
                    pool.dma_start(out[m], x3[:]).then_inc(stored, 16)
                    pool.wait_ge(stored, 16 * m + 16)
                    pool.sem_inc(x3_free, 1)

            steps(step, pool)
            pool.wait_ge(stored, 16 * NG)

        @block.tensor
        def _(pe):
            def project(slot, moving):
                return pe.matmul(side_bank[:, :], w[:, slot, :], moving, start=True, stop=True)

            def project_v(slot, source):
                for t in range(TILES):
                    mm = pe.matmul(side_bank[:, t * P:(t + 1) * P], source[:, t * P:(t + 1) * P],
                                   w[:, slot, :], start=True, stop=True)
                return mm

            def turn(dst, source):
                for t in range(TILES):
                    mm = pe.transpose(dst[:, t * P:(t + 1) * P], source(t), ident[:])
                return mm

            def half_scores(dst, t, half, a, rows, blocks, mask):
                if a == "B":
                    for b in range(2):
                        pe.matmul(dst[64 * b:64 * b + 64, :].rearrange("p (h k) -> p h k", k=S),
                                  masks[:, 0, :], mask.unsqueeze(1).to_broadcast([P, 8, S]),
                                  start=True, stop=False, skip_group_check=True)
                for gg in range(2):
                    g = 2 * half + gg
                    for b in range(2):
                        lo = t * P + 64 * b
                        mm = pe.matmul(dst[64 * b:64 * b + 64, gg * 256:gg * 256 + 256],
                                       rows[a][:, g, lo:lo + 64], blocks[a][:, g, :, lo:lo + 64],
                                       start=(a == "A"), stop=True, skip_group_check=True)
                return mm

            def scores(n, a, t):
                for half in range(2):
                    if t > 0:
                        pe.wait_ge(max_ready[a], 8 * n + 2 * t + half - 1)
                    half_scores(score_bank[half], t, half, a, q_rows, k_block, masks[:, 1, :])\
                        .then_inc(scores_written[a], 1)

            def turn_maxima(n, a):
                pe.wait_ge(max_ready[a], 8 * n + 8)
                for t in range(TILES):
                    mm = pe.transpose(side_bank[0:H, t * P:(t + 1) * P], neg_max[a][:, t, :], ident[:])
                mm.then_inc(max_turned[a], 1)

            def t_scores(n, a, t):
                if t == 0:
                    pe.wait_ge(max_stacked[a], 64 * n + 64)
                for half in range(2):
                    if t > 0:
                        pe.wait_ge(probs_ready[a], 8 * n + 2 * t + half - 1)
                    half_scores(t_bank[half], t, half, a, k_rows, q_block, masks[:, 2, :])\
                        .then_inc(t_written[a], 1)

            def context(n, a, t):
                for i in range(2):
                    pe.wait_ge(probs_ready[a], 8 * n + 2 * t + i + 1)
                    if t == 2 and i == 0:
                        pe.wait_ge(ctx_kept[a], 2 * n + 1)
                    pairs = range(4 * i, 4 * i + 4)
                    for p in pairs:
                        c, at = p % 4, (t % 2) * 256 + i * P
                        mo = pe.matmul(ctx_bank[32 * c:32 * c + 32, at:at + P], v_block[a][:, t, p, :],
                                       probs[:, t % 2, p * P:(p + 1) * P], start=True, stop=True,
                                       skip_group_check=True)
                    if t % 2 == 1 and i == 1:
                        mo.then_inc(ctx_written[a], 1)
                    for p in pairs:
                        c = p % 4
                        md = pe.matmul(den_bank[32 * c:32 * c + 32, 0:P], den_ones[:, 2 * t + i, :],
                                       probs[:, t % 2, p * P:(p + 1) * P], start=(t == 0 and i == 0),
                                       stop=(t == TILES - 1 and i == 1), skip_group_check=True)
                md.then_inc(probs_used[a], 1)

            def spread_sums(n, a, u):
                if u == 0:
                    pe.wait_ge(inv_ready[a], n + 1)
                else:
                    pe.wait_ge(ctx_n_ready[a], 2 * n + 1)
                for k in range(4):
                    mm = pe.matmul(y_bank[:, k * P:(k + 1) * P], spread[:, 4 * u + k, :],
                                   inv_den[:], start=True, stop=True)
                mm.then_inc(spread_written[a], 1)

            def out_project(n, a, slot):
                pe.wait_ge(ctx_n_ready[a], 2 * n + 2)
                for t in range(TILES):
                    for ih in range(4):
                        for b in range(2):
                            i, r2 = ih // 2, ih % 2
                            mm = pe.matmul(y_bank[64 * b:64 * b + 64, t * P:(t + 1) * P],
                                           ctx_n[:, t, ih * 64:ih * 64 + 64],
                                           w[:, slot + 4 * i + 2 * b + r2, :],
                                           start=(ih == 0), stop=(ih == 3), skip_group_check=True)
                mm.then_inc(y_written[a], 1)

            def expert(n, e):
                pe.wait_ge(gated_ready, (E + 1) * n + e + 1)
                mm = pe.matmul(ctx_bank[:, :], w[:, W_2 + e, :], gated[:, e % 2, :],
                               start=(e == 0), stop=(e == E))
                mm.then_inc(gated_used if e < E else sum_written, 1)

            def hidden(n, e):
                if e >= 2:
                    pe.wait_ge(silu_ready, (E + 1) * n + e - 1)
                pe.matmul(t_bank[e % 2][:, :], w[:, W_1 + e, :], x2t[:], start=True, stop=True)\
                  .then_inc(h_written, 1)

            def spread_gate(n, e):
                pe.matmul(score_bank[e % 2][:, :], pick[0:96, e, :], gate_t[0:96, :], start=True, stop=True)\
                  .then_inc(gates_written, 1)

            def step(n, a, b, nxt):
                m = n - 1
                if a:
                    pe.wait_ge(q_stacked["A"], STACK * n + STACK)
                    pe.wait_ge(k_stacked["A"], STACK * n + STACK)
                    scores(n, "A", 0)
                    scores(n, "A", 1)
                if nxt:
                    pe.wait_ge(xt_in, 16 * n + 32)
                    if b:
                        pe.wait_ge(roped_ready, 4 * n)
                    project(W_QA, xt[:]).then_inc(q_written["A"], 1)
                if a:
                    scores(n, "A", 2)
                if nxt:
                    pe.wait_ge(split_ready["A"], 2 * n + 3)
                    project(W_KA, xt[:]).then_inc(k_written["A"], 1)
                if a:
                    scores(n, "A", 3)
                if b:
                    pe.wait_ge(q_stacked["B"], STACK * m + STACK)
                    pe.wait_ge(k_stacked["B"], STACK * m + STACK)
                    if a:
                        pe.wait_ge(max_ready["A"], 8 * n + 8)
                    scores(m, "B", 0)
                if a:
                    if nxt:
                        pe.wait_ge(split_ready["A"], 2 * n + 4)
                    turn_maxima(n, "A")
                if b:
                    scores(m, "B", 1)
                    scores(m, "B", 2)
                if a:
                    pe.wait_ge(v_placed["A"], 2 * n + 2)
                    t_scores(n, "A", 0)
                if b:
                    scores(m, "B", 3)
                if a:
                    t_scores(n, "A", 1)
                    context(n, "A", 0)
                if b:
                    if a:
                        pe.wait_ge(max_t_ready["A"], n + 1)
                    turn_maxima(m, "B")
                if a:
                    t_scores(n, "A", 2)
                    context(n, "A", 1)
                    t_scores(n, "A", 3)
                    context(n, "A", 2)
                if b:
                    if a:
                        pe.wait_ge(probs_ready["A"], 8 * n + 8)
                    t_scores(m, "B", 0)
                if a:
                    context(n, "A", 3)
                    if b:
                        pe.wait_ge(max_t_ready["B"], m + 1)
                    else:
                        pe.wait_ge(max_t_ready["A"], n + 1)
                    pe.wait_ge(ct_in, 16 * n + 16)
                    project(W_KB, ct[:]).then_inc(k_written["B"], 1)
                if b:
                    t_scores(m, "B", 1)
                if a:
                    pe.wait_ge(roped_ready, 4 * n + 1)
                    project(W_KBR, ct[:]).then_inc(k_written["B"], 1)
                    spread_sums(n, "A", 0)
                if b:
                    if a:
                        pe.wait_ge(ctx_kept["A"], 2 * n + 2)
                    context(m, "B", 0)
                    t_scores(m, "B", 2)
                if a:
                    spread_sums(n, "A", 1)
                if b:
                    context(m, "B", 1)
                    t_scores(m, "B", 3)
                if a:
                    out_project(n, "A", W_OA)
                if b:
                    context(m, "B", 2)
                    context(m, "B", 3)
                if a:
                    pe.wait_ge(roped_ready, 4 * n + 2)
                    project_v(W_VB, ct).then_inc(v_written["B"], 1)
                if nxt:
                    pe.wait_ge(v_placed["B"], 2 * n + 2)
                    project_v(W_VA, xt).then_inc(v_written["A"], 1)
                if b:
                    if a:
                        pe.wait_ge(res_ready["A"], n + 1)
                    spread_sums(m, "B", 0)
                    spread_sums(m, "B", 1)
                if a:
                    if nxt:
                        pe.wait_ge(v_placed["A"], 2 * n + 4)
                    else:
                        pe.wait_ge(v_placed["B"], 2 * n + 2)
                    pe.wait_ge(normed["A"], n + 1)
                    turn(side_bank, lambda t: x1[:, t, :]).then_inc(x_turned["A"], 1)
                if b:
                    out_project(m, "B", W_OB)
                if a:
                    pe.wait_ge(xt_ready["A"], n + 1)
                    project(W_QB, x1t[:]).then_inc(q_written["B"], 1)
                    pe.wait_ge(roped_ready, 4 * n + 3)
                    project(W_QBR, x1t[:]).then_inc(q_written["B"], 1)
                if b:
                    if a:
                        pe.wait_ge(roped_ready, 4 * n + 4)
                    pe.wait_ge(normed["B"], m + 1)
                    turn(side_bank, lambda t: x2[:, t, :]).then_inc(x_turned["B"], 1)
                    pe.wait_ge(xt_ready["B"], m + 1)
                    for t in range(TILES):
                        mm = pe.matmul(den_bank[:, t * (E + 1):(t + 1) * (E + 1)],
                                       x2t[:, t * P:(t + 1) * P], rw[:], start=True, stop=True)
                    mm.then_inc(logits_written, 1)
                    hidden(m, 0)
                    hidden(m, 1)
                    pe.wait_ge(gate_step, 4 * m + 4)
                    for t in range(TILES):
                        mm = pe.transpose(den_bank[0:96, :].bitcast(BF16)[:, t * P:(t + 1) * P],
                                          gate3[:, t, :], ident16[:])
                    mm.then_inc(gate_turned, 1)
                    pe.wait_ge(gate_t_ready, m + 1)
                    spread_gate(m, 0)
                    spread_gate(m, 1)
                    for e in range(E + 1):
                        if e + 2 <= E:
                            hidden(m, e + 2)
                        elif e + 2 == E + 1:
                            pe.wait_ge(silu_ready, (E + 1) * m + E)
                            pe.matmul(t_bank[1][:, :], w[:, W_UP, :], x2t[:], start=True, stop=True)\
                              .then_inc(up_written, 1)
                        expert(m, e)
                        if e + 2 <= E:
                            spread_gate(m, e + 2)
                    pe.wait_ge(yt_ready, m + 1)
                    turn(y_bank, lambda t: yt[:, t * P:(t + 1) * P]).then_inc(out_turned, 1)

            pe.wait_ge(loaded, 16 * N_LOADS)
            pe.wait_ge(zeroed["A"], ZERO_FILLS)
            pe.wait_ge(zeroed["B"], ZERO_FILLS)
            pe.wait_ge(xt_in, 16)
            project(W_QA, xt[:]).then_inc(q_written["A"], 1)
            pe.wait_ge(split_ready["A"], 1)
            project(W_KA, xt[:]).then_inc(k_written["A"], 1)
            pe.wait_ge(split_ready["A"], 2)
            project_v(W_VA, xt).then_inc(v_written["A"], 1)
            pe.wait_ge(v_placed["A"], 2)
            steps(step, pe)

        @block.scalar
        def _(act):
            def hi_part(part):
                act.copy(split[part + "A"][:, 0, :], side_bank[:, :]).then_inc(hi_ready["A"], 1)

            def maxima(a):
                act.copy(neg_max_t[a][:], side_bank[0:H, :]).then_inc(max_t_ready[a], 1)

            def exps(n, a, t):
                for half in range(2):
                    act.wait_ge(t_written[a], 8 * n + 2 * t + half + 1)
                    act.activation(probs[:, t % 2, half * 512:half * 512 + 512], t_bank[half][:, :],
                                   ACT.Exp, scale=SCALE).then_inc(probs_ready[a], 1)

            def keep_context(n, a, u):
                act.wait_ge(ctx_written[a], 2 * n + u + 1)
                act.copy(ctx_raw[:, 2 * u:2 * u + 2, :].rearrange("p t c -> p (t c)"), ctx_bank[:, :])\
                   .then_inc(ctx_kept[a], 1)

            def step(n, a, b, nxt):
                m = n - 1
                if nxt:
                    act.wait_ge(spilled["A"], 32 * n + 32)
                    act.wait_ge(q_written["A"], n + 2)
                    hi_part("q")
                    act.wait_ge(k_written["A"], n + 2)
                    hi_part("k")
                if a:
                    act.wait_ge(max_turned["A"], n + 1)
                    maxima("A")
                    exps(n, "A", 0)
                    exps(n, "A", 1)
                if b:
                    act.wait_ge(max_turned["B"], m + 1)
                    maxima("B")
                if a:
                    act.wait_ge(probs_used["A"], 4 * n + 1)
                    exps(n, "A", 2)
                    keep_context(n, "A", 0)
                    act.wait_ge(probs_used["A"], 4 * n + 2)
                    exps(n, "A", 3)
                if b:
                    if a:
                        act.wait_ge(probs_used["A"], 4 * n + 3)
                    exps(m, "B", 0)
                if a:
                    keep_context(n, "A", 1)
                    act.wait_ge(rope_sum_ready, 2 * n + 1)
                    if b:
                        act.wait_ge(spilled["B"], 32 * n)
                    act.copy(split["kB"][:, 0, :], rope_sum[:]).then_inc(hi_ready["B"], 1)
                if b:
                    if a:
                        act.wait_ge(probs_used["A"], 4 * n + 4)
                    exps(m, "B", 1)
                    act.wait_ge(probs_used["B"], 4 * m + 1)
                    exps(m, "B", 2)
                    if a:
                        act.wait_ge(ctx_n_ready["A"], 2 * n + 2)
                    keep_context(m, "B", 0)
                    act.wait_ge(probs_used["B"], 4 * m + 2)
                    exps(m, "B", 3)
                    keep_context(m, "B", 1)
                if a:
                    act.wait_ge(x_turned["A"], n + 1)
                    act.copy(x1t[:], side_bank[:, :]).then_inc(xt_ready["A"], 1)
                    act.wait_ge(rope_sum_ready, 2 * n + 2)
                    act.copy(split["qB"][:, 0, :], rope_sum[:]).then_inc(hi_ready["B"], 1)
                if b:
                    act.wait_ge(x_turned["B"], m + 1)
                    act.copy(x2t[:], side_bank[:, :]).then_inc(xt_ready["B"], 1)
                    act.wait_ge(logit_ready, m + 1)
                    act.activation(small[0][:], small[1][:], ACT.Exp).then_inc(exp_ready, 1)
                    act.activation(col[0][:].unsqueeze(2), logit[:, :, E:E + 1], ACT.Exp, scale=-1.0)\
                       .then_inc(exp_ready, 1)
                    for e in range(E + 1):
                        act.wait_ge(h_written, (E + 1) * m + e + 1)
                        if e >= 2:
                            act.wait_ge(gated_ready, (E + 1) * m + e - 1)
                        act.activation(act_h[:, e % 2, :], t_bank[e % 2][:, :], ACT.Silu)\
                           .then_inc(silu_ready, 1)
                        if e == 1:
                            act.wait_ge(gate_turned, m + 1)
                            act.copy(gate_t[0:96, :], den_bank[0:96, :].bitcast(BF16)[:, 0:G])\
                               .then_inc(gate_t_ready, 1)
                    act.wait_ge(sum_written, m + 1)
                    act.copy(yt[:], ctx_bank[:, :]).then_inc(yt_ready, 1)

            act.wait_ge(q_written["A"], 1)
            hi_part("q")
            act.wait_ge(k_written["A"], 1)
            hi_part("k")
            steps(step, act)

        @block.vector
        def _(dve):
            def lo_part(part):
                buf = split[part + "A"]
                dve.tensor_tensor(buf[:, 1, :], side_bank[:, :], buf[:, 0, :], ALU.subtract)\
                   .then_inc(split_ready["A"], 1)

            def place_v(a):
                for b in range(2):
                    dst = v_block[a][64 * b:64 * b + 64, :, :, 16 * b:16 * b + 16]
                    src = side_bank[64 * b:64 * b + 64, :].rearrange("p (t c d) -> p t c d", t=TILES, d=16)
                    if a == "A":
                        dve.tensor_copy(dst, src).then_inc(v_placed[a], 1)
                    else:
                        bv = rows3[64 * b:64 * b + 64, 0, :].rearrange("p (c d) -> p c d", d=16)
                        for t in range(TILES):
                            ins = dve.tensor_tensor(dst[:, t], src[:, t], bv, ALU.add)
                        ins.then_inc(v_placed[a], 1)

            def rotate(s, col_b):
                dve.scalar_tensor_tensor(
                    out=roped[:, s, :].rearrange("p (b s) -> p b s", s=S),
                    in0=side_bank[:, :].rearrange("p (b s) -> p b s", s=S),
                    scalar=bias[:, col_b:col_b + 1],
                    in1=rows3[:, 2:3, S * s:S * s + S].to_broadcast([P, G // S, S]),
                    op0=ALU.add, op1=ALU.mult).then_inc(roped_ready, 1)

            def maxima(n, a, t):
                for half in range(2):
                    dve.wait_ge(scores_written[a], 8 * n + 2 * t + half + 1)
                    dve.tensor_reduce(
                        neg_max[a][:, t, :].rearrange("p (r g) -> p g r", r=4)[:, 2 * half:2 * half + 2, :],
                        score_bank[half][:, :].rearrange("p (g r k) -> p g r k", g=2, k=S),
                        AX_X, ALU.max, negate=True).then_inc(max_ready[a], 1)

            def normalise(n, a):
                for u in range(2):
                    dve.wait_ge(ctx_kept[a], 2 * n + u + 1)
                    dve.wait_ge(spread_written[a], 2 * n + u + 1)
                    dve.tensor_tensor(ctx_n[:, 2 * u:2 * u + 2, :].rearrange("p t c -> p (t c)"),
                                      y_bank[:, :],
                                      ctx_raw[:, 2 * u:2 * u + 2, :].rearrange("p t c -> p (t c)"),
                                      ALU.mult).then_inc(ctx_n_ready[a], 1)

            def add_norm(n, j, residual, dst):
                dve.tensor_tensor(res[:].rearrange("p t d -> p (t d)"), y_bank[:, :],
                                  residual[:].rearrange("p t d -> p (t d)"), ALU.add)\
                   .then_inc(res_ready[j], 1)
                dve.wait_ge(res_ready[j], n + 1)
                for t in range(TILES):
                    dve.bn_stats(stats[:, t, :], res[:, t, :]).then_inc(stats_ready[j], 1)
                dve.wait_ge(stats_ready[j], 4 * n + 4)
                if not isinstance(n, int):
                    dve.sem_inc(carried, 1)
                for t in range(TILES):
                    dve.bn_aggr(mean_var[:, t, :], stats[:, t, :]).then_inc(var_ready[j], 1)
                dve.wait_ge(rstd_ready[j], n + 1)
                for t in range(TILES):
                    ins = dve.tensor_scalar(dst[:, t, :], res[:, t, :], mean_var[:, t, 0:1],
                                            rstd[:, t:t + 1], ALU.subtract, ALU.mult)
                ins.then_inc(normed[j], 1)

            def bc(a):
                return a.to_broadcast([P, TILES, E])

            def router_gates(n):
                done = [0]

                def chain(ins):
                    done[0] += 1
                    ins.then_inc(router_step, 1)
                    dve.wait_ge(router_step, ROUTER * n + done[0])

                dve.wait_ge(logits_written, n + 1)
                chain(dve.tensor_copy(logit[:].rearrange("p t e -> p (t e)"),
                                      den_bank[:, 0:TILES * (E + 1)]))
                if not isinstance(n, int):
                    dve.sem_inc(carried, 1)
                for t in range(TILES):
                    last = dve.max(top[:, t, :], logit[:, t, 0:E])
                chain(last)
                lg, first, second = logit[:, :, 0:E], top[:, :, 0:1], top[:, :, 1:2]
                dve.tensor_tensor(small[1][:], lg, bc(first), ALU.subtract).then_inc(logit_ready, 1)
                chain(dve.tensor_tensor(small[2][:], lg, bc(second), ALU.is_gt))
                chain(dve.tensor_tensor(small[3][:], lg, bc(second), ALU.is_equal))
                chain(dve.tensor_tensor_scan(small[4][:].rearrange("p t e -> p (t e)"),
                                             seg[:].rearrange("p t e -> p (t e)"),
                                             small[3][:].rearrange("p t e -> p (t e)"), 0.0,
                                             ALU.mult, ALU.add))
                chain(dve.tensor_tensor(col[1][:].unsqueeze(2), first, second, ALU.is_gt))
                chain(dve.tensor_scalar(col[1][:], col[1][:], -1.0, 2.0, ALU.mult, ALU.add))
                chain(dve.tensor_tensor(small[4][:], small[4][:], bc(col[1][:].unsqueeze(2)), ALU.is_le))
                chain(dve.tensor_tensor(small[4][:], small[4][:], small[3][:], ALU.mult))
                chain(dve.tensor_tensor(small[4][:], small[4][:], small[2][:], ALU.add))
                dve.wait_ge(exp_ready, 2 * n + 2)
                chain(dve.tensor_reduce(col[2][:], small[0][:], AX_X, ALU.add))
                chain(dve.reciprocal(col[2][:], col[2][:]))
                chain(dve.tensor_tensor(small[4][:], small[4][:], small[0][:], ALU.mult))
                chain(dve.tensor_tensor(gate[:, :, 0:E], small[4][:], bc(col[2][:].unsqueeze(2)), ALU.mult))
                chain(dve.tensor_scalar(col[3][:], col[0][:], 1.0, None, ALU.add))
                chain(dve.reciprocal(gate[:, :, E:E + 1], col[3][:].unsqueeze(2)))
                assert done[0] == ROUTER
                dve.tensor_copy(gate3[:, :, 0:E + 1], gate[:]).then_inc(gate_step, 1)
                dve.wait_ge(gate_step, 4 * n + 1)
                dve.tensor_tensor(gate_r[:, 0], gate[:], gate3[:, :, 0:E + 1], ALU.subtract)\
                   .then_inc(gate_step, 1)
                dve.wait_ge(gate_step, 4 * n + 2)
                dve.tensor_copy(gate3[:, :, 32:32 + E + 1], gate_r[:, 0]).then_inc(gate_step, 1)
                dve.wait_ge(gate_step, 4 * n + 3)
                dve.tensor_tensor(gate3[:, :, 64:64 + E + 1], gate_r[:, 0], gate3[:, :, 32:32 + E + 1],
                                  ALU.subtract).then_inc(gate_step, 1)

            def experts(n):
                for e in range(E + 1):
                    dve.wait_ge(silu_ready, (E + 1) * n + e + 1)
                    src = act_h[:, e % 2, :]
                    if e == E:
                        dve.wait_ge(up_written, n + 1)
                        dve.tensor_tensor(sh_h[:], t_bank[1][:, :], src, ALU.mult).then_inc(sh_ready, 1)
                        dve.wait_ge(sh_ready, n + 1)
                        src = sh_h[:]
                    if e >= 2:
                        dve.wait_ge(gated_used, E * n + e - 1)
                    dve.wait_ge(gates_written, (E + 1) * n + e + 1)
                    dve.tensor_tensor(gated[:, e % 2, :], score_bank[e % 2][:, :], src, ALU.mult)\
                       .then_inc(gated_ready, 1)

            def step(n, a, b, nxt):
                m = n - 1
                if a:
                    maxima(n, "A", 0)
                    maxima(n, "A", 1)
                if nxt:
                    dve.wait_ge(hi_ready["A"], 2 * n + 3)
                    lo_part("q")
                if a:
                    maxima(n, "A", 2)
                if nxt:
                    dve.wait_ge(hi_ready["A"], 2 * n + 4)
                    lo_part("k")
                if a:
                    maxima(n, "A", 3)
                if b:
                    for t in range(TILES):
                        maxima(m, "B", t)
                if a:
                    dve.wait_ge(k_written["B"], 2 * n + 1)
                    rotate(0, 2)
                    dve.wait_ge(k_written["B"], 2 * n + 2)
                    rotate(1, 3)
                    dve.wait_ge(probs_used["A"], 4 * n + 4)
                    dve.reciprocal(inv_den[:], den_bank[:, 0:P]).then_inc(inv_ready["A"], 1)
                    normalise(n, "A")
                    dve.wait_ge(xn_in, 16 * n + 16)
                    dve.wait_ge(y_written["A"], n + 1)
                    add_norm(n, "A", xn, x1)
                if b:
                    dve.wait_ge(probs_used["B"], 4 * m + 4)
                    dve.reciprocal(inv_den[:], den_bank[:, 0:P]).then_inc(inv_ready["B"], 1)
                if a:
                    dve.wait_ge(v_written["B"], n + 1)
                    place_v("B")
                if nxt:
                    dve.wait_ge(v_written["A"], n + 2)
                    place_v("A")
                if b:
                    normalise(m, "B")
                if a:
                    dve.wait_ge(rope_sum_ready, 2 * n + 1)
                    dve.wait_ge(q_written["B"], 2 * n + 1)
                    rotate(0, 0)
                    dve.wait_ge(q_written["B"], 2 * n + 2)
                    rotate(1, 1)
                if b:
                    dve.wait_ge(biased, m + 1)
                    dve.wait_ge(y_written["B"], m + 1)
                    add_norm(m, "B", x1b, x2)
                    router_gates(m)
                    experts(m)
                    dve.wait_ge(out_turned, m + 1)
                    dve.wait_ge(x3_free, m + 1)
                    add_norm(m, "C", x2, x3)

            for a in "AB":
                dve.memset(k_block[a][:], 0.0).then_inc(zeroed[a], 1)
                dve.memset(q_rows[a][96:128], 0.0).then_inc(zeroed[a], 1)
                dve.memset(v_block[a][:], 0.0).then_inc(zeroed[a], 1)
                dve.memset(k_rows[a][96:128], 0.0).then_inc(rows_zero, 1)
                dve.wait_ge(rows_zero, 1 if a == "A" else 2)
                dve.memset(k_rows[a][96:100], 1.0).then_inc(zeroed[a], 1)
            dve.wait_ge(loaded, 16 * N_LOADS)
            dve.wait_ge(pool_const, 5)
            dve.wait_ge(hi_ready["A"], 1)
            lo_part("q")
            dve.wait_ge(hi_ready["A"], 2)
            lo_part("k")
            dve.wait_ge(v_written["A"], 1)
            place_v("A")
            steps(step, dve)


def constants():
    bfloat16 = mybir.dt.np(BF16)
    half = DH // 2
    freq = 1.0 / 10000.0 ** (np.arange(half, dtype=np.float32) / half)
    angle = np.arange(S, dtype=np.float32)[None, :] * np.float32(freq)[:, None]
    cos, sin = np.cos(angle).astype(np.float32), np.sin(angle).astype(np.float32)
    rope = np.concatenate([np.tile(np.concatenate([cos, cos]), (H, 1)),
                           np.tile(np.concatenate([-sin, sin]), (H, 1))], axis=1)
    masks = np.zeros((P, 3, S), np.float32)
    masks[:S, 0] = np.eye(S)
    masks[:S, 1] = np.where(np.arange(S)[None, :] > np.arange(S)[:, None], MASKED, 0.0)
    masks[:S, 2] = np.where(np.arange(S)[:, None] > np.arange(S)[None, :], MASKED, 0.0)
    den_ones = np.zeros((P, TILES, 2, 2, TILES, 2, 2), np.float32)
    spread = np.zeros((4, 32, TILES, 2, 4, 2, 16), np.float32)
    for t in range(TILES):
        for i in range(2):
            for b in range(2):
                den_ones[64 * b:64 * b + 64, t, i, :, t, b, i] = 1.0
                for c in range(4):
                    spread[c, 4 * t + 2 * b + i, t, i, c, b, :] = 1.0
    pick = np.zeros((P, E + 1, P), np.float32)
    for s in range(3):
        for e in range(E + 1):
            pick[32 * s + e, e] = 1.0
    return dict(rope=rope, c_ident=np.eye(P, dtype=np.float32), c_ident16=np.eye(P).astype(bfloat16),
                c_masks=masks.astype(bfloat16), c_den_ones=den_ones.reshape(P, 8, 32),
                c_spread=spread.reshape(P, 8, P), c_pick=pick.astype(bfloat16))


def kernel(**inputs):
    import concourse.bacc as bacc
    from concourse.bass_utils import run_bass_kernel_spmd

    a = {k: np.ascontiguousarray(v) for k, v in inputs.items()}
    x = a["x"].reshape(NG, TILES, P, D)
    group_t = lambda v: np.ascontiguousarray(v.reshape(NG, G, D).transpose(0, 2, 1))

    def swap_halves(m):
        return m.reshape(H, 2, DH // 2, -1)[:, ::-1].reshape(D, -1)

    def out_slices(m):
        rows = m.T.reshape(2, 4, 2, DH, D)
        slots = np.zeros((2, 2, 2, 4, 2, 2, DH, D), m.dtype)
        for b in range(2):
            for r2 in range(2):
                slots[:, b, r2, :, b, r2] = rows[:, :, r2]
        return slots.reshape(8, P, D)

    q_w, k_w, v_w = a["L0_xattn_q_w"], a["L0_xattn_k_w"], a["L0_xattn_v_w"]
    gate_up = a["L0_ffn_shared_gate_up"]
    slots = [a["L0_attn_w_qkv"][i * D:(i + 1) * D].T for i in range(3)]
    slots += [q_w.T, swap_halves(q_w).T, k_w.T, swap_halves(k_w).T, v_w.T]
    slots += [*a["L0_ffn_w1"], gate_up[:, :D], gate_up[:, D:], *a["L0_ffn_w2"], a["L0_ffn_shared_down"]]
    slots += [*out_slices(a["L0_attn_w_out"]), *out_slices(a["L0_xattn_o_w"])]
    consts = constants()
    q_b, k_b = a["L0_xattn_q_b"].reshape(D, 1), a["L0_xattn_k_b"].reshape(D, 1)
    row_consts = np.stack([np.broadcast_to(a["L0_xattn_v_b"], (P, D)), np.broadcast_to(a["L0_xattn_o_b"], (P, D)),
                           consts.pop("rope")], axis=1)
    arrays = dict(
        x=np.ascontiguousarray(x.transpose(0, 2, 1, 3)), x_t=group_t(a["x"]), ctx_t=group_t(a["ctx_1024"]),
        weights=np.ascontiguousarray(np.stack(slots, axis=1)),
        router=np.concatenate([a["L0_ffn_router_w"], a["L0_ffn_shared_gate_w"]], axis=1),
        row_consts=row_consts,
        biases=np.concatenate([q_b, swap_halves(q_b), k_b, swap_halves(k_b)], axis=1), **consts)

    nc = bacc.Bacc("TRN2", target_bir_lowering=False, num_devices=1)
    aps = {k: nc.dram_tensor("in_" + k, v.shape, mybir.dt.from_np(v.dtype), kind="ExternalInput").ap()
           for k, v in arrays.items()}
    out = nc.dram_tensor("out", (NG, P, TILES, D), F32, kind="ExternalOutput").ap()
    decoder_layer(nc, out=out, **aps)
    result = run_bass_kernel_spmd(nc, [{"in_" + k: v for k, v in arrays.items()}], core_ids=[0])
    got = result.results[0]["out"]
    return np.ascontiguousarray(got.transpose(0, 2, 1, 3)).reshape(S, S, D)
```

```python
from contextlib import ExitStack

import numpy as np

import concourse.bass as bass
from concourse import mybir

ALU = mybir.AluOpType
ACT = mybir.ActivationFunctionType
F32 = mybir.dt.float32
F16 = mybir.dt.float16
BF16 = mybir.dt.bfloat16
AX_X = mybir.AxisListType.X

P = 128
D = 128
H, DH, S = 16, 8, 64
TOKENS = 64 * S
TILES = 4
G = TILES * P
NG = TOKENS // G
E = 8
PAIRS = H // 2
BANKS = 8
MASKED = -1.0e30
EPS = 1e-5
SCALE = float(DH) ** -0.5
INV_SCALE = 64.0

W_QA, W_KA, W_VA, W_QB, W_QBR, W_KB, W_KBR, W_VB = range(8)
W_1 = 8
W_GATE, W_UP = W_1 + E, W_1 + E + 1
W_2 = W_UP + 1
W_DOWN = W_2 + E
W_OA = W_DOWN + 1
W_OB = W_OA + 4
NW = W_OB + 4

ROUTER = 16
STACK = 16 * 15
N_LOADS = 11
ZERO_FILLS = 5


def decoder_layer(nc, x, x_t, ctx_t, weights, router, row_consts, biases, c_ident, c_masks,
                  c_den_ones, c_spread, c_own_head, out):
    ctx = ExitStack()
    with ctx:
        def sb(name, shape, dt=F32):
            return ctx.enter_context(nc.sbuf_tensor(name, shape, dt))

        def sem(name):
            return ctx.enter_context(nc.semaphore(name))

        w = sb("w", [P, NW, D])
        rw = sb("rw", [P, E + 1])
        rows3 = sb("rows3", [P, 3, D])
        bias = sb("bias", [P, 4])
        ident = sb("ident", [P, P])
        masks = sb("masks", [P, 4, S], BF16)
        den_ones = sb("den_ones", [P, 8, 32])
        spread = sb("spread", [P, 8, P], F16)
        own_head = sb("own_head", [P, P])
        half_neg = sb("half_neg", [P, TILES])
        seg = sb("seg", [P, TILES, E])
        xt = sb("xt", [P, G])
        ct = sb("ct", [P, G])
        xn = sb("xn", [P, TILES, D])
        split = {n: sb("split_" + n, [P, 2, G], F16) for n in ("qA", "kA", "qB", "kB")}
        q_rows = {a: sb("q_rows" + a, [P, 4, G], F16) for a in "AB"}
        k_rows = {a: sb("k_rows" + a, [P, 4, G], F16) for a in "AB"}
        q_block = {a: sb("q_block" + a, [P, 4, 4, G], F16) for a in "AB"}
        k_block = {a: sb("k_block" + a, [P, 4, 4, G], F16) for a in "AB"}
        v_block = {a: sb("v_block" + a, [P, TILES, PAIRS, 32]) for a in "AB"}
        neg_max = {a: sb("neg_max" + a, [P, TILES, H]) for a in "AB"}
        neg_max_t = {a: sb("neg_max_t" + a, [H, G], F16) for a in "AB"}
        probs = sb("probs", [P, 2, H * S])
        ctx_raw = sb("ctx_raw", [P, TILES, 256])
        inv_den = sb("inv_den", [P, P])
        inv_own = sb("inv_own", [P, P])
        inv_hi, inv_lo = sb("inv_hi", [P, P], F16), sb("inv_lo", [P, P], F16)
        ctx_n = sb("ctx_n", [P, TILES, 2, 2, S])
        ctx_s = sb("ctx_s", [P, TILES, 2, S])
        roped = sb("roped", [P, 2, G])
        rope_sum = sb("rope_sum", [P, G])
        res = sb("res", [P, TILES, D])
        stats = sb("stats", [P, TILES, 6])
        mean_var = sb("mean_var", [P, TILES, 2])
        rstd = sb("rstd", [P, TILES])
        veps = sb("veps", [P, TILES])
        eps = sb("eps", [P, TILES])
        x1 = sb("x1", [P, TILES, D])
        x1b = sb("x1b", [P, TILES, D])
        x1t = sb("x1t", [P, G])
        x2 = sb("x2", [P, TILES, D])
        x2t = sb("x2t", [P, G])
        x3 = sb("x3", [P, TILES, D])
        logit = sb("logit", [P, TILES, E + 1])
        top = sb("top", [P, TILES, 8])
        small = [sb(f"small{k}", [P, TILES, E]) for k in range(6)]
        col = [sb(f"col{k}", [P, TILES]) for k in range(4)]
        gate = sb("gate", [P, TILES, E + 1])
        act_h = sb("act_h", [P, 2, G])
        sh_h = sb("sh_h", [P, G])
        moe_sum = sb("moe_sum", [P, TILES, D])

        bank = [ctx.enter_context(nc.psum_tensor(f"bank{i}", [P, 512], F32)) for i in range(BANKS)]
        scratch = {a: nc.dram_tensor("split_" + a, [4, P, G], F16).ap() for a in "AB"}

        score_bank, t_bank = bank[0:2], bank[2:4]
        ctx_bank, y_bank, den_bank, side_bank = bank[4], bank[5], bank[6], bank[7]
        expert_bank = bank[4:6]

        def per_attention(name):
            return {a: sem(name + a) for a in "AB"}

        loaded, pool_const, rows_zero = sem("weights_loaded"), sem("pool_const"), sem("rows_zero")
        zeroed = per_attention("zeroed")
        carried = sem("waits_carried")
        first_xt_in = sem("first_xt_in")
        xt_in, ct_in, xn_in, stored = sem("xt_in"), sem("ct_in"), sem("xn_in"), sem("stored")
        q_written, k_written = per_attention("q_written"), per_attention("k_written")
        v_written, v_placed = per_attention("v_written"), per_attention("v_placed")
        hi_ready, split_ready = per_attention("hi_ready"), per_attention("split_ready")
        spilled = per_attention("spilled")
        q_stacked, k_stacked = per_attention("q_stacked"), per_attention("k_stacked")
        roped_ready, rope_sum_ready = sem("roped_ready"), sem("rope_sum_ready")
        scores_written, max_ready = per_attention("scores_written"), per_attention("max_ready")
        max_turned, max_t_ready = per_attention("max_turned"), per_attention("max_t_ready")
        max_stacked = per_attention("max_stacked")
        t_written, probs_ready = per_attention("t_written"), per_attention("probs_ready")
        probs_used = per_attention("probs_used")
        ctx_written, ctx_kept = per_attention("ctx_written"), per_attention("ctx_kept")
        inv_step, inv_ready = per_attention("inv_step"), per_attention("inv_ready")
        spread_written, ctx_n_ready = per_attention("spread_written"), per_attention("ctx_n_ready")
        ctx_s_ready = per_attention("ctx_s_ready")
        y_written, x_turned, xt_ready = (per_attention("y_written"), per_attention("x_turned"),
                                         per_attention("xt_ready"))
        norms = "ABC"
        res_ready, rstd_ready, normed = ({a: sem(name + a) for a in norms}
                                         for name in ("res_ready", "rstd_ready", "normed"))
        stats_ready, var_ready = ({a: sem(name + a) for a in norms} for name in ("stats_ready", "var_ready"))
        veps_ready = {a: sem("veps_ready" + a) for a in norms}
        biased = sem("biased")
        logits_written, logit_ready, exp_ready = sem("logits_written"), sem("logit_ready"), sem("exp_ready")
        router_step, gates_ready = sem("router_step"), sem("gates_ready")
        h_written, silu_ready = sem("h_written"), sem("silu_ready")
        up_written, sh_ready = sem("up_written"), sem("sh_ready")
        x3_free = sem("x3_free")
        expert_written, expert_added = sem("expert_written"), sem("expert_added")

        block = ctx.enter_context(nc.Block())

        def steps(step, eng):
            step(0, a=True, b=False, c=False, nxt=True)
            step(1, a=True, b=True, c=False, nxt=True)
            with eng.Fori(2, NG - 1) as n:
                step(n, a=True, b=True, c=True, nxt=True)
            step(NG - 1, a=True, b=True, c=True, nxt=False)
            step(NG, a=False, b=True, c=True, nxt=False)
            step(NG + 1, a=False, b=False, c=True, nxt=False)

        @block.sync
        def _(sp):
            sp.dma_start(xt[:], x_t[0]).then_inc(first_xt_in, 16)
            sp.dma_start(w[:, 0:W_1], weights[:, 0:W_1]).then_inc(loaded, 16)
            for dst, src in ((rw, router), (rows3, row_consts), (bias, biases), (ident, c_ident),
                             (masks, c_masks), (den_ones, c_den_ones), (spread, c_spread),
                             (own_head, c_own_head)):
                sp.dma_start(dst[:], src).then_inc(loaded, 16)
            sp.dma_start(ct[:], ctx_t[0]).then_inc(ct_in, 16)
            sp.dma_start(xn[:], x[0]).then_inc(xn_in, 16)
            sp.dma_start(w[:, W_OA:NW], weights[:, W_OA:NW]).then_inc(loaded, 16)
            sp.dma_start(w[:, W_1:W_OA], weights[:, W_1:W_OA]).then_inc(loaded, 16)

            def carry(n):
                if not isinstance(n, int):
                    sp.sem_inc(carried, 1)

            def stack(a, part):
                base = 0 if part == "q" else 2
                order = (0, 0, 1) if part == "q" else (0, 1, 0)
                rows, blocks = (q_rows, q_block) if part == "q" else (k_rows, k_block)
                done = (q_stacked if part == "q" else k_stacked)[a]
                for s, hl in enumerate(order):
                    src = scratch[a][base + hl].rearrange("(g r) t -> r g t", g=4)
                    sp.dma_start(rows[a][32 * s:32 * s + 32], src).then_inc(done, 16)
                    for r in range(4):
                        sp.dma_start(blocks[a][32 * s + 8 * r:32 * s + 8 * r + 8, :, r, :],
                                     src[8 * r:8 * r + 8]).then_inc(done, 16)

            def spill(a, part):
                base = 0 if part == "q" else 2
                sp.dma_start(scratch[a][base:base + 2].rearrange("s p t -> p s t"),
                             split[part + a][:]).then_inc(spilled[a], 16)

            def maxima(a):
                for r in range(4):
                    sp.dma_start(q_block[a][96 + r:97 + r, :, r, :],
                                 neg_max_t[a][4 * r:4 * r + 4]).then_inc(max_stacked[a], 16)

            def step(n, a, b, c, nxt):
                m = n - 1
                if a:
                    sp.wait_ge(max_t_ready["A"], n + 1)
                    carry(n)
                    maxima("A")
                if nxt:
                    sp.wait_ge(q_stacked["A"], STACK * n + STACK)
                    carry(n)
                    sp.wait_ge(split_ready["A"], 2 * n + 3)
                    carry(n)
                    spill("A", "q")
                    sp.wait_ge(k_stacked["A"], STACK * n + STACK)
                    carry(n)
                    sp.wait_ge(split_ready["A"], 2 * n + 4)
                    carry(n)
                    spill("A", "k")
                if b:
                    sp.wait_ge(max_t_ready["B"], m + 1)
                    carry(n)
                    maxima("B")
                if nxt:
                    sp.wait_ge(spilled["A"], 32 * n + 64)
                    carry(n)
                    sp.wait_ge(t_written["A"], 8 * n + 8)
                    carry(n)
                    stack("A", "q")
                    stack("A", "k")
                if a:
                    sp.wait_ge(split_ready["B"], 2 * n + 1)
                    carry(n)
                    if b:
                        sp.wait_ge(k_stacked["B"], STACK * n)
                        carry(n)
                    spill("B", "k")
                    sp.wait_ge(spilled["B"], 32 * n + 16)
                    carry(n)
                    if b:
                        sp.wait_ge(t_written["B"], 8 * m + 8)
                        carry(n)
                    stack("B", "k")
                if nxt:
                    sp.wait_ge(res_ready["A"], n + 1)
                    carry(n)
                    sp.dma_start(xn[:], x[n + 1]).then_inc(xn_in, 16)
                    sp.wait_ge(v_written["B"], n + 1)
                    carry(n)
                    sp.dma_start(ct[:], ctx_t[n + 1]).then_inc(ct_in, 16)
                if a:
                    sp.wait_ge(split_ready["B"], 2 * n + 2)
                    carry(n)
                    if b:
                        sp.wait_ge(q_stacked["B"], STACK * n)
                        carry(n)
                    spill("B", "q")
                    sp.wait_ge(spilled["B"], 32 * n + 32)
                    carry(n)
                    stack("B", "q")

            sp.wait_ge(zeroed["A"], ZERO_FILLS)
            sp.wait_ge(zeroed["B"], ZERO_FILLS)
            sp.wait_ge(split_ready["A"], 1)
            spill("A", "q")
            sp.wait_ge(split_ready["A"], 2)
            spill("A", "k")
            sp.wait_ge(spilled["A"], 32)
            stack("A", "q")
            stack("A", "k")
            steps(step, sp)

        @block.gpsimd
        def _(pool):
            for a in "AB":
                pool.memset(q_block[a][:], 0.0).then_inc(zeroed[a], 1)
            pool.memset(half_neg[:], -0.5).then_inc(pool_const, 1)
            pool.memset(eps[:], EPS).then_inc(pool_const, 1)
            pool.memset(seg[:], 1.0).then_inc(pool_const, 1)
            pool.wait_ge(pool_const, 3)
            pool.memset(seg[:, :, 0:1], 0.0).then_inc(pool_const, 1)
            pool.wait_ge(loaded, 16 * N_LOADS)
            pool.sem_inc(x3_free, 1)

            def rope_sum_and_lo(n, part, k):
                pool.wait_ge(roped_ready, 4 * n + 2 * k)
                pool.tensor_tensor(rope_sum[:], roped[:, 0, :], roped[:, 1, :], ALU.add)\
                    .then_inc(rope_sum_ready, 1)
                pool.wait_ge(rope_sum_ready, 2 * n + k)
                pool.wait_ge(hi_ready["B"], 2 * n + k)
                pool.tensor_tensor(split[part + "B"][:, 1, :], rope_sum[:], split[part + "B"][:, 0, :],
                                   ALU.subtract).then_inc(split_ready["B"], 1)

            def inverse_root(n, j):
                pool.wait_ge(var_ready[j], 4 * n + 4)
                pool.tensor_tensor(veps[:], mean_var[:, :, 1], eps[:], ALU.add).then_inc(veps_ready[j], 1)
                pool.wait_ge(veps_ready[j], n + 1)
                pool.tensor_tensor(rstd[:], veps[:], half_neg[:], ALU.pow).then_inc(rstd_ready[j], 1)

            def bias_residual(n):
                pool.wait_ge(normed["A"], n + 1)
                pool.tensor_tensor(x1b[:], x1[:], rows3[:, 1:2, :].to_broadcast([P, TILES, D]), ALU.add)\
                    .then_inc(biased, 1)

            def step(n, a, b, c, nxt):
                m, k = n - 1, n - 2
                if nxt:
                    pool.wait_ge(v_written["A"], n + 1)
                    pool.dma_start(xt[:], x_t[n + 1]).then_inc(xt_in, 16)
                if c:
                    inverse_root(k, "C")
                    pool.wait_ge(normed["C"], k + 1)
                    pool.dma_start(out[k], x3[:]).then_inc(stored, 16)
                if a:
                    rope_sum_and_lo(n, "k", 1)
                if c:
                    pool.wait_ge(stored, 16 * k + 16)
                    pool.sem_inc(x3_free, 1)
                if a:
                    inverse_root(n, "A")
                    rope_sum_and_lo(n, "q", 2)
                if b:
                    inverse_root(m, "B")
                    pool.wait_ge(res_ready["B"], m + 1)
                if a:
                    bias_residual(n)

            steps(step, pool)
            pool.wait_ge(stored, 16 * NG)

        @block.tensor
        def _(pe):
            def project(slot, moving):
                return pe.matmul(side_bank[:, :], w[:, slot, :], moving, start=True, stop=True)

            def project_v(slot, source):
                for t in range(TILES):
                    mm = pe.matmul(side_bank[:, t * P:(t + 1) * P], source[:, t * P:(t + 1) * P],
                                   w[:, slot, :], start=True, stop=True)
                return mm

            def turn(dst, source):
                for t in range(TILES):
                    mm = pe.transpose(dst[:, t * P:(t + 1) * P], source(t), ident[:])
                return mm

            def half_scores(dst, t, half, a, rows, blocks, mask):
                if a == "B":
                    pe.matmul(dst[:, :].rearrange("p (h k) -> p h k", k=S),
                              masks[:, 0:2, :].rearrange("p b q -> p (b q)"),
                              mask.unsqueeze(1).to_broadcast([P, 8, S]),
                              start=True, stop=False, skip_group_check=True)
                for gg in range(2):
                    g = 2 * half + gg
                    for b in range(2):
                        lo = t * P + 64 * b
                        mm = pe.matmul(dst[64 * b:64 * b + 64, gg * 256:gg * 256 + 256],
                                       rows[a][:, g, lo:lo + 64], blocks[a][:, g, :, lo:lo + 64],
                                       start=(a == "A"), stop=True, skip_group_check=True)
                return mm

            def scores(n, a, t):
                for half in range(2):
                    if t > 0:
                        pe.wait_ge(max_ready[a], 8 * n + 2 * t + half - 1)
                    half_scores(score_bank[half], t, half, a, q_rows, k_block, masks[:, 2, :])\
                        .then_inc(scores_written[a], 1)

            def turn_maxima(n, a):
                pe.wait_ge(max_ready[a], 8 * n + 8)
                for t in range(TILES):
                    mm = pe.transpose(side_bank[0:H, t * P:(t + 1) * P], neg_max[a][:, t, :], ident[:])
                mm.then_inc(max_turned[a], 1)

            def t_scores(n, a, t):
                if t == 0:
                    pe.wait_ge(max_stacked[a], 64 * n + 64)
                for half in range(2):
                    if t > 0:
                        pe.wait_ge(probs_ready[a], 8 * n + 2 * t + half - 1)
                    half_scores(t_bank[half], t, half, a, k_rows, q_block, masks[:, 3, :])\
                        .then_inc(t_written[a], 1)

            def context(n, a, t):
                for i in range(2):
                    pe.wait_ge(probs_ready[a], 8 * n + 2 * t + i + 1)
                    if t == 2 and i == 0:
                        pe.wait_ge(ctx_kept[a], 2 * n + 1)
                    pairs = range(4 * i, 4 * i + 4)
                    for p in pairs:
                        c, at = p % 4, (t % 2) * 256 + i * P
                        mo = pe.matmul(ctx_bank[32 * c:32 * c + 32, at:at + P], v_block[a][:, t, p, :],
                                       probs[:, t % 2, p * P:(p + 1) * P], start=True, stop=True,
                                       skip_group_check=True)
                    if t % 2 == 1 and i == 1:
                        mo.then_inc(ctx_written[a], 1)
                    for p in pairs:
                        c = p % 4
                        md = pe.matmul(den_bank[32 * c:32 * c + 32, 0:P], den_ones[:, 2 * t + i, :],
                                       probs[:, t % 2, p * P:(p + 1) * P], start=(t == 0 and i == 0),
                                       stop=(t == TILES - 1 and i == 1), skip_group_check=True)
                md.then_inc(probs_used[a], 1)

            def spread_sums(n, a, u):
                if u == 0:
                    pe.wait_ge(inv_ready[a], 2 * n + 2)
                else:
                    pe.wait_ge(ctx_n_ready[a], 2 * n + 1)
                for k in range(4):
                    for part in (inv_hi, inv_lo):
                        mm = pe.matmul(y_bank[:, k * P:(k + 1) * P], spread[:, 4 * u + k, :], part[:],
                                       start=(part is inv_hi), stop=(part is inv_lo))
                mm.then_inc(spread_written[a], 1)

            def out_project(n, a, slot):
                pe.wait_ge(ctx_s_ready[a], 2 * n + 2)
                for t in range(TILES):
                    for i in range(2):
                        for b in range(2):
                            mm = pe.matmul(y_bank[64 * b:64 * b + 64, t * P:(t + 1) * P],
                                           ctx_s[:, t, i, :], w[:, slot + 2 * i + b, :],
                                           start=(i == 0), stop=(i == 1), skip_group_check=True)
                mm.then_inc(y_written[a], 1)

            def expert(n, e):
                if e < E:
                    pe.wait_ge(silu_ready, (E + 1) * n + e + 1)
                    source = act_h[:, e % 2, :]
                else:
                    pe.wait_ge(sh_ready, n + 1)
                    source = sh_h[:]
                if e >= 2:
                    pe.wait_ge(expert_added, (E + 1) * n + e - 1)
                elif e == 0:
                    pe.wait_ge(ctx_kept["B"], 2 * n + 2)
                else:
                    pe.wait_ge(res_ready["B"], n + 1)
                for t in range(TILES):
                    mm = pe.matmul(expert_bank[e % 2][:, t * P:(t + 1) * P], source[:, t * P:(t + 1) * P],
                                   w[:, W_2 + e, :], start=True, stop=True)
                mm.then_inc(expert_written, 1)

            def hidden(n, e):
                if e >= 2:
                    pe.wait_ge(silu_ready, (E + 1) * n + e - 1)
                pe.matmul(t_bank[e % 2][:, :], w[:, W_1 + e, :], x2t[:], start=True, stop=True)\
                  .then_inc(h_written, 1)

            def up(n):
                pe.wait_ge(silu_ready, (E + 1) * n + E)
                pe.matmul(t_bank[1][:, :], w[:, W_UP, :], x2t[:], start=True, stop=True)\
                  .then_inc(up_written, 1)

            def step(n, a, b, c, nxt):
                m, k = n - 1, n - 2
                if c:
                    pe.wait_ge(xt_ready["B"], k + 1)
                    hidden(k, 0)
                    hidden(k, 1)
                if a:
                    if not b:
                        pe.wait_ge(v_placed["A"], 2 * n + 2)
                    turn_maxima(n, "A")
                if nxt:
                    pe.wait_ge(xt_in, 16 * n + 16)
                    pe.wait_ge(max_t_ready["A"], n + 1)
                    project(W_QA, xt[:]).then_inc(q_written["A"], 1)
                if c:
                    expert(k, 0)
                    hidden(k, 2)
                    expert(k, 1)
                    hidden(k, 3)
                if nxt:
                    pe.wait_ge(split_ready["A"], 2 * n + 3)
                    project(W_KA, xt[:]).then_inc(k_written["A"], 1)
                if c:
                    expert(k, 2)
                    hidden(k, 4)
                if b:
                    pe.wait_ge(q_stacked["B"], STACK * m + STACK)
                    pe.wait_ge(k_stacked["B"], STACK * m + STACK)
                    if a:
                        pe.wait_ge(max_ready["A"], 8 * n + 8)
                for t in range(TILES):
                    if b:
                        scores(m, "B", t)
                    if c:
                        expert(k, 3 + t)
                        hidden(k, 5 + t)
                if b:
                    if nxt:
                        pe.wait_ge(split_ready["A"], 2 * n + 4)
                    elif a:
                        pe.wait_ge(max_t_ready["A"], n + 1)
                    turn_maxima(m, "B")
                if c:
                    expert(k, 7)
                    up(k)
                    expert(k, 8)
                if a:
                    if c:
                        pe.wait_ge(silu_ready, (E + 1) * k + E + 1)
                    t_scores(n, "A", 0)
                    t_scores(n, "A", 1)
                    pe.wait_ge(v_placed["A"], 2 * n + 2)
                    if c:
                        pe.wait_ge(expert_added, (E + 1) * k + E + 1)
                    context(n, "A", 0)
                    t_scores(n, "A", 2)
                    context(n, "A", 1)
                    t_scores(n, "A", 3)
                    if b:
                        pe.wait_ge(max_t_ready["B"], m + 1)
                    elif nxt:
                        pe.wait_ge(split_ready["A"], 2 * n + 4)
                    pe.wait_ge(ct_in, 16 * n + 16)
                    project(W_KB, ct[:]).then_inc(k_written["B"], 1)
                    context(n, "A", 2)
                if b:
                    if a:
                        pe.wait_ge(probs_ready["A"], 8 * n + 8)
                    elif c:
                        pe.wait_ge(expert_added, (E + 1) * k + E + 1)
                    t_scores(m, "B", 0)
                if a:
                    context(n, "A", 3)
                    pe.wait_ge(roped_ready, 4 * n + 1)
                    project(W_KBR, ct[:]).then_inc(k_written["B"], 1)
                if b:
                    t_scores(m, "B", 1)
                if a:
                    spread_sums(n, "A", 0)
                if b:
                    if a:
                        pe.wait_ge(ctx_kept["A"], 2 * n + 2)
                    context(m, "B", 0)
                    t_scores(m, "B", 2)
                if a:
                    spread_sums(n, "A", 1)
                if b:
                    context(m, "B", 1)
                    t_scores(m, "B", 3)
                if a:
                    out_project(n, "A", W_OA)
                if b:
                    context(m, "B", 2)
                    context(m, "B", 3)
                if a:
                    pe.wait_ge(roped_ready, 4 * n + 2)
                    project_v(W_VB, ct).then_inc(v_written["B"], 1)
                if b:
                    if a:
                        pe.wait_ge(res_ready["A"], n + 1)
                    spread_sums(m, "B", 0)
                if a:
                    pe.wait_ge(v_placed["B"], 2 * n + 2)
                    pe.wait_ge(normed["A"], n + 1)
                    turn(side_bank, lambda t: x1[:, t, :]).then_inc(x_turned["A"], 1)
                if b:
                    spread_sums(m, "B", 1)
                if a:
                    pe.wait_ge(xt_ready["A"], n + 1)
                    project(W_QB, x1t[:]).then_inc(q_written["B"], 1)
                if nxt:
                    pe.wait_ge(q_stacked["A"], STACK * n + 2 * STACK)
                    pe.wait_ge(k_stacked["A"], STACK * n + 2 * STACK)
                    if b:
                        pe.wait_ge(max_ready["B"], 8 * m + 8)
                    else:
                        pe.wait_ge(max_ready["A"], 8 * n + 8)
                    scores(n + 1, "A", 0)
                if a:
                    pe.wait_ge(roped_ready, 4 * n + 3)
                    project(W_QBR, x1t[:]).then_inc(q_written["B"], 1)
                if nxt:
                    scores(n + 1, "A", 1)
                    scores(n + 1, "A", 2)
                if b:
                    out_project(m, "B", W_OB)
                if nxt:
                    pe.wait_ge(roped_ready, 4 * n + 4)
                    project_v(W_VA, xt).then_inc(v_written["A"], 1)
                    scores(n + 1, "A", 3)
                if b:
                    if nxt:
                        pe.wait_ge(v_placed["A"], 2 * n + 4)
                    elif a:
                        pe.wait_ge(roped_ready, 4 * n + 4)
                    pe.wait_ge(normed["B"], m + 1)
                    turn(side_bank, lambda t: x2[:, t, :]).then_inc(x_turned["B"], 1)
                    pe.wait_ge(xt_ready["B"], m + 1)
                    for t in range(TILES):
                        mm = pe.matmul(den_bank[:, t * (E + 1):(t + 1) * (E + 1)],
                                       x2t[:, t * P:(t + 1) * P], rw[:], start=True, stop=True)
                    mm.then_inc(logits_written, 1)

            pe.wait_ge(loaded, 16 * N_LOADS)
            pe.wait_ge(zeroed["A"], ZERO_FILLS)
            pe.wait_ge(zeroed["B"], ZERO_FILLS)
            pe.wait_ge(first_xt_in, 16)
            project(W_QA, xt[:]).then_inc(q_written["A"], 1)
            pe.wait_ge(split_ready["A"], 1)
            project(W_KA, xt[:]).then_inc(k_written["A"], 1)
            pe.wait_ge(split_ready["A"], 2)
            project_v(W_VA, xt).then_inc(v_written["A"], 1)
            pe.wait_ge(v_placed["A"], 2)
            pe.wait_ge(q_stacked["A"], STACK)
            pe.wait_ge(k_stacked["A"], STACK)
            for t in range(TILES):
                scores(0, "A", t)
            steps(step, pe)

        @block.scalar
        def _(act):
            def hi_part(part):
                act.copy(split[part + "A"][:, 0, :], side_bank[:, :]).then_inc(hi_ready["A"], 1)

            def maxima(a):
                act.copy(neg_max_t[a][:], side_bank[0:H, :]).then_inc(max_t_ready[a], 1)

            def exps(n, a, t):
                for half in range(2):
                    act.wait_ge(t_written[a], 8 * n + 2 * t + half + 1)
                    act.activation(probs[:, t % 2, half * 512:half * 512 + 512], t_bank[half][:, :],
                                   ACT.Exp, scale=SCALE).then_inc(probs_ready[a], 1)

            def keep_context(n, a, u):
                act.wait_ge(ctx_written[a], 2 * n + u + 1)
                act.copy(ctx_raw[:, 2 * u:2 * u + 2, :].rearrange("p t c -> p (t c)"), ctx_bank[:, :])\
                   .then_inc(ctx_kept[a], 1)

            def silu(n, e):
                act.wait_ge(h_written, (E + 1) * n + e + 1)
                if e >= 2:
                    act.wait_ge(expert_written, (E + 1) * n + e - 1)
                act.activation(act_h[:, e % 2, :], t_bank[e % 2][:, :], ACT.Silu).then_inc(silu_ready, 1)

            def step(n, a, b, c, nxt):
                m, k = n - 1, n - 2
                if c:
                    silu(k, 0)
                if a:
                    act.wait_ge(max_turned["A"], n + 1)
                    maxima("A")
                if nxt:
                    act.wait_ge(spilled["A"], 32 * n + 32)
                    act.wait_ge(q_written["A"], n + 2)
                    hi_part("q")
                if c:
                    silu(k, 1)
                    silu(k, 2)
                    silu(k, 3)
                if nxt:
                    act.wait_ge(k_written["A"], n + 2)
                    hi_part("k")
                if c:
                    for e in range(4, E + 1):
                        silu(k, e)
                if b:
                    act.wait_ge(max_turned["B"], m + 1)
                    maxima("B")
                if a:
                    exps(n, "A", 0)
                    exps(n, "A", 1)
                    act.wait_ge(probs_used["A"], 4 * n + 1)
                    exps(n, "A", 2)
                    keep_context(n, "A", 0)
                    act.wait_ge(probs_used["A"], 4 * n + 2)
                    exps(n, "A", 3)
                if b:
                    if a:
                        act.wait_ge(probs_used["A"], 4 * n + 3)
                    exps(m, "B", 0)
                if a:
                    keep_context(n, "A", 1)
                if b:
                    if a:
                        act.wait_ge(probs_used["A"], 4 * n + 4)
                    exps(m, "B", 1)
                if a:
                    act.wait_ge(rope_sum_ready, 2 * n + 1)
                    if b:
                        act.wait_ge(spilled["B"], 32 * n)
                    act.copy(split["kB"][:, 0, :], rope_sum[:]).then_inc(hi_ready["B"], 1)
                if b:
                    act.wait_ge(probs_used["B"], 4 * m + 1)
                    exps(m, "B", 2)
                    if a:
                        act.wait_ge(ctx_n_ready["A"], 2 * n + 2)
                    keep_context(m, "B", 0)
                    act.wait_ge(probs_used["B"], 4 * m + 2)
                    exps(m, "B", 3)
                    keep_context(m, "B", 1)
                if a:
                    act.wait_ge(x_turned["A"], n + 1)
                    act.copy(x1t[:], side_bank[:, :]).then_inc(xt_ready["A"], 1)
                    act.wait_ge(rope_sum_ready, 2 * n + 2)
                    act.copy(split["qB"][:, 0, :], rope_sum[:]).then_inc(hi_ready["B"], 1)
                if b:
                    act.wait_ge(x_turned["B"], m + 1)
                    act.copy(x2t[:], side_bank[:, :]).then_inc(xt_ready["B"], 1)
                    act.wait_ge(logit_ready, m + 1)
                    act.activation(small[0][:], small[1][:], ACT.Exp).then_inc(exp_ready, 1)
                    act.activation(col[0][:].unsqueeze(2), logit[:, :, E:E + 1], ACT.Exp, scale=-1.0)\
                       .then_inc(exp_ready, 1)

            act.wait_ge(q_written["A"], 1)
            hi_part("q")
            act.wait_ge(k_written["A"], 1)
            hi_part("k")
            steps(step, act)

        @block.vector
        def _(dve):
            def lo_part(part):
                buf = split[part + "A"]
                dve.tensor_tensor(buf[:, 1, :], side_bank[:, :], buf[:, 0, :], ALU.subtract)\
                   .then_inc(split_ready["A"], 1)

            def place_v(a):
                for b in range(2):
                    dst = v_block[a][64 * b:64 * b + 64, :, :, 16 * b:16 * b + 16]
                    src = side_bank[64 * b:64 * b + 64, :].rearrange("p (t c d) -> p t c d", t=TILES, d=16)
                    if a == "A":
                        dve.tensor_copy(dst, src).then_inc(v_placed[a], 1)
                    else:
                        bv = rows3[64 * b:64 * b + 64, 0, :].rearrange("p (c d) -> p c d", d=16)
                        for t in range(TILES):
                            ins = dve.tensor_tensor(dst[:, t], src[:, t], bv, ALU.add)
                        ins.then_inc(v_placed[a], 1)

            def rotate(s, col_b):
                dve.scalar_tensor_tensor(
                    out=roped[:, s, :].rearrange("p (b s) -> p b s", s=S),
                    in0=side_bank[:, :].rearrange("p (b s) -> p b s", s=S),
                    scalar=bias[:, col_b:col_b + 1],
                    in1=rows3[:, 2:3, S * s:S * s + S].to_broadcast([P, G // S, S]),
                    op0=ALU.add, op1=ALU.mult).then_inc(roped_ready, 1)

            def maxima(n, a, t):
                for half in range(2):
                    dve.wait_ge(scores_written[a], 8 * n + 2 * t + half + 1)
                    dve.tensor_reduce(
                        neg_max[a][:, t, :].rearrange("p (r g) -> p g r", r=4)[:, 2 * half:2 * half + 2, :],
                        score_bank[half][:, :].rearrange("p (g r k) -> p g r k", g=2, k=S),
                        AX_X, ALU.max, negate=True).then_inc(max_ready[a], 1)

            def inverse_sums(n, a):
                dve.wait_ge(probs_used[a], 4 * n + 4)
                dve.reciprocal(inv_den[:], den_bank[:, 0:P]).then_inc(inv_step[a], 1)
                dve.wait_ge(inv_step[a], 2 * n + 1)
                dve.tensor_tensor(inv_own[:], inv_den[:], own_head[:], ALU.mult).then_inc(inv_step[a], 1)
                dve.wait_ge(inv_step[a], 2 * n + 2)
                dve.tensor_copy(inv_hi[:], inv_own[:]).then_inc(inv_ready[a], 1)
                dve.wait_ge(inv_ready[a], 2 * n + 1)
                dve.tensor_tensor(inv_lo[:], inv_own[:], inv_hi[:], ALU.subtract).then_inc(inv_ready[a], 1)

            def normalise(n, a):
                for u in range(2):
                    tiles = slice(2 * u, 2 * u + 2)
                    dve.wait_ge(ctx_kept[a], 2 * n + u + 1)
                    dve.wait_ge(spread_written[a], 2 * n + u + 1)
                    dve.tensor_tensor(ctx_n[:, tiles].rearrange("p t i r q -> p (t i r q)"), y_bank[:, :],
                                      ctx_raw[:, tiles, :].rearrange("p t c -> p (t c)"),
                                      ALU.mult).then_inc(ctx_n_ready[a], 1)
                    dve.wait_ge(ctx_n_ready[a], 2 * n + u + 1)
                    dve.tensor_tensor(ctx_s[:, tiles], ctx_n[:, tiles, :, 0, :], ctx_n[:, tiles, :, 1, :],
                                      ALU.add).then_inc(ctx_s_ready[a], 1)

            def statistics(n, j, source):
                for t in range(TILES):
                    dve.bn_stats(stats[:, t, :], source[:, t, :]).then_inc(stats_ready[j], 1)
                dve.wait_ge(stats_ready[j], 4 * n + 4)
                if not isinstance(n, int):
                    dve.sem_inc(carried, 1)
                for t in range(TILES):
                    dve.bn_aggr(mean_var[:, t, :], stats[:, t, :]).then_inc(var_ready[j], 1)

            def normed_rows(n, j, source, dst):
                dve.wait_ge(rstd_ready[j], n + 1)
                for t in range(TILES):
                    ins = dve.tensor_scalar(dst[:, t, :], source[:, t, :], mean_var[:, t, 0:1],
                                            rstd[:, t:t + 1], ALU.subtract, ALU.mult)
                ins.then_inc(normed[j], 1)

            def add_residual(n, j, residual):
                dve.wait_ge(y_written[j], n + 1)
                dve.tensor_tensor(res[:].rearrange("p t d -> p (t d)"), y_bank[:, :],
                                  residual[:].rearrange("p t d -> p (t d)"), ALU.add)\
                   .then_inc(res_ready[j], 1)
                dve.wait_ge(res_ready[j], n + 1)
                statistics(n, j, res)

            def bc(a):
                return a.to_broadcast([P, TILES, E])

            def router_gates(n):
                done = [0]

                def chain(ins):
                    done[0] += 1
                    ins.then_inc(router_step, 1)
                    dve.wait_ge(router_step, ROUTER * n + done[0])

                dve.wait_ge(logits_written, n + 1)
                chain(dve.tensor_copy(logit[:].rearrange("p t e -> p (t e)"),
                                      den_bank[:, 0:TILES * (E + 1)]))
                if not isinstance(n, int):
                    dve.sem_inc(carried, 1)
                for t in range(TILES):
                    last = dve.max(top[:, t, :], logit[:, t, 0:E])
                chain(last)
                lg, first, second = logit[:, :, 0:E], top[:, :, 0:1], top[:, :, 1:2]
                dve.tensor_tensor(small[1][:], lg, bc(first), ALU.subtract).then_inc(logit_ready, 1)
                chain(dve.tensor_tensor(small[2][:], lg, bc(second), ALU.is_gt))
                chain(dve.tensor_tensor(small[3][:], lg, bc(second), ALU.is_equal))
                chain(dve.tensor_tensor_scan(small[4][:].rearrange("p t e -> p (t e)"),
                                             seg[:].rearrange("p t e -> p (t e)"),
                                             small[3][:].rearrange("p t e -> p (t e)"), 0.0,
                                             ALU.mult, ALU.add))
                chain(dve.tensor_tensor(col[1][:].unsqueeze(2), first, second, ALU.is_gt))
                chain(dve.tensor_scalar(col[1][:], col[1][:], -1.0, 2.0, ALU.mult, ALU.add))
                chain(dve.tensor_tensor(small[4][:], small[4][:], bc(col[1][:].unsqueeze(2)), ALU.is_le))
                chain(dve.tensor_tensor(small[4][:], small[4][:], small[3][:], ALU.mult))
                chain(dve.tensor_tensor(small[4][:], small[4][:], small[2][:], ALU.add))
                dve.wait_ge(exp_ready, 2 * n + 2)
                chain(dve.tensor_reduce(col[2][:], small[0][:], AX_X, ALU.add))
                chain(dve.reciprocal(col[2][:], col[2][:]))
                chain(dve.tensor_tensor(small[4][:], small[4][:], small[0][:], ALU.mult))
                chain(dve.tensor_tensor(gate[:, :, 0:E], small[4][:], bc(col[2][:].unsqueeze(2)), ALU.mult))
                chain(dve.tensor_scalar(col[3][:], col[0][:], 1.0, None, ALU.add))
                chain(dve.reciprocal(gate[:, :, E:E + 1], col[3][:].unsqueeze(2)))
                assert done[0] == ROUTER

            def add_expert(n, e):
                if e == E:
                    dve.wait_ge(silu_ready, (E + 1) * n + E + 1)
                    dve.wait_ge(up_written, n + 1)
                    dve.tensor_tensor(sh_h[:], t_bank[1][:, :], act_h[:, E % 2, :], ALU.mult)\
                       .then_inc(sh_ready, 1)
                if e > 0:
                    dve.wait_ge(expert_added, (E + 1) * n + e)
                dve.wait_ge(expert_written, (E + 1) * n + e + 1)
                before = x2 if e == 0 else moe_sum
                for t in range(TILES):
                    ins = dve.scalar_tensor_tensor(
                        out=moe_sum[:, t, :], in0=expert_bank[e % 2][:, t * P:(t + 1) * P],
                        scalar=gate[:, t, e:e + 1], in1=before[:, t, :], op0=ALU.mult, op1=ALU.add)
                ins.then_inc(expert_added, 1)

            def step(n, a, b, c, nxt):
                m, k = n - 1, n - 2
                if c:
                    add_expert(k, 0)
                if nxt:
                    dve.wait_ge(hi_ready["A"], 2 * n + 3)
                    lo_part("q")
                if c:
                    add_expert(k, 1)
                if nxt:
                    dve.wait_ge(hi_ready["A"], 2 * n + 4)
                    lo_part("k")
                if c:
                    add_expert(k, 2)
                for t in range(TILES):
                    if b:
                        maxima(m, "B", t)
                    if c:
                        add_expert(k, 3 + t)
                if c:
                    add_expert(k, 7)
                    add_expert(k, 8)
                    dve.wait_ge(expert_added, (E + 1) * k + E + 1)
                    dve.wait_ge(x3_free, k + 1)
                    statistics(k, "C", moe_sum)
                if a:
                    dve.wait_ge(k_written["B"], 2 * n + 1)
                    rotate(0, 2)
                if c:
                    normed_rows(k, "C", moe_sum, x3)
                if a:
                    dve.wait_ge(k_written["B"], 2 * n + 2)
                    rotate(1, 3)
                    inverse_sums(n, "A")
                    normalise(n, "A")
                    dve.wait_ge(xn_in, 16 * n + 16)
                    add_residual(n, "A", xn)
                if b:
                    inverse_sums(m, "B")
                if a:
                    normed_rows(n, "A", res, x1)
                    dve.wait_ge(v_written["B"], n + 1)
                    place_v("B")
                if b:
                    normalise(m, "B")
                if a:
                    dve.wait_ge(rope_sum_ready, 2 * n + 1)
                    dve.wait_ge(q_written["B"], 2 * n + 1)
                    rotate(0, 0)
                if nxt:
                    maxima(n + 1, "A", 0)
                if a:
                    dve.wait_ge(q_written["B"], 2 * n + 2)
                    rotate(1, 1)
                if nxt:
                    maxima(n + 1, "A", 1)
                    maxima(n + 1, "A", 2)
                if b:
                    dve.wait_ge(biased, m + 1)
                    add_residual(m, "B", x1b)
                if nxt:
                    dve.wait_ge(v_written["A"], n + 2)
                    place_v("A")
                if b:
                    normed_rows(m, "B", res, x2)
                if nxt:
                    maxima(n + 1, "A", 3)
                if b:
                    router_gates(m)

            for a in "AB":
                dve.memset(k_block[a][:], 0.0).then_inc(zeroed[a], 1)
                dve.memset(q_rows[a][96:128], 0.0).then_inc(zeroed[a], 1)
                dve.memset(v_block[a][:], 0.0).then_inc(zeroed[a], 1)
                dve.memset(k_rows[a][96:128], 0.0).then_inc(rows_zero, 1)
                dve.wait_ge(rows_zero, 1 if a == "A" else 2)
                dve.memset(k_rows[a][96:100], 1.0).then_inc(zeroed[a], 1)
            dve.wait_ge(loaded, 16 * N_LOADS)
            dve.wait_ge(pool_const, 4)
            dve.wait_ge(hi_ready["A"], 1)
            lo_part("q")
            dve.wait_ge(hi_ready["A"], 2)
            lo_part("k")
            dve.wait_ge(v_written["A"], 1)
            place_v("A")
            for t in range(TILES):
                maxima(0, "A", t)
            steps(step, dve)


def constants():
    half = DH // 2
    freq = 1.0 / 10000.0 ** (np.arange(half, dtype=np.float32) / half)
    angle = np.arange(S, dtype=np.float32)[None, :] * np.float32(freq)[:, None]
    cos, sin = np.cos(angle).astype(np.float32), np.sin(angle).astype(np.float32)
    rope = np.concatenate([np.tile(np.concatenate([cos, cos]), (H, 1)),
                           np.tile(np.concatenate([-sin, sin]), (H, 1))], axis=1)
    masks = np.zeros((P, 4, S), np.float32)
    masks[:S, 0] = masks[:S, 1] = np.eye(S)
    masks[:S, 2] = np.where(np.arange(S)[None, :] > np.arange(S)[:, None], MASKED, 0.0)
    masks[:S, 3] = np.where(np.arange(S)[:, None] > np.arange(S)[None, :], MASKED, 0.0)
    den_ones = np.zeros((P, TILES, 2, 2, TILES, 2, 2), np.float32)
    spread = np.zeros((4, 2, 16, TILES, 2, 4, 2, 2, DH), np.float16)
    own_head = np.zeros((4, 2, 16, 2, S), np.float32)
    for x in range(2):
        own_head[:, x, :, x] = INV_SCALE
    for t in range(TILES):
        for i in range(2):
            for b in range(2):
                den_ones[64 * b:64 * b + 64, t, i, :, t, b, i] = 1.0
                for c in range(4):
                    for x in range(2):
                        spread[c, x, 4 * t + 2 * b + i, t, i, c, b, x] = 1.0 / INV_SCALE
    return dict(rope=rope, c_ident=np.eye(P, dtype=np.float32),
                c_masks=masks.astype(mybir.dt.np(BF16)), c_den_ones=den_ones.reshape(P, 8, 32),
                c_spread=spread.reshape(P, 8, P), c_own_head=own_head.reshape(P, P))


def kernel(**inputs):
    import concourse.bacc as bacc
    from concourse.bass_utils import run_bass_kernel_spmd

    a = {k: np.ascontiguousarray(v) for k, v in inputs.items()}
    x = a["x"].reshape(NG, TILES, P, D)
    group_t = lambda v: np.ascontiguousarray(v.reshape(NG, G, D).transpose(0, 2, 1))

    def swap_halves(m):
        return m.reshape(H, 2, DH // 2, -1)[:, ::-1].reshape(D, -1)

    def out_slices(m):
        rows = m.T.reshape(2, 4, 2, DH, D)
        slots = np.zeros((2, 2, 4, 2, 2, DH, D), m.dtype)
        for b in range(2):
            slots[:, b, :, b] = rows
        return slots.reshape(4, P, D)

    q_w, k_w, v_w = a["L0_xattn_q_w"], a["L0_xattn_k_w"], a["L0_xattn_v_w"]
    gate_up = a["L0_ffn_shared_gate_up"]
    slots = [a["L0_attn_w_qkv"][i * D:(i + 1) * D].T for i in range(3)]
    slots += [q_w.T, swap_halves(q_w).T, k_w.T, swap_halves(k_w).T, v_w.T]
    slots += [*a["L0_ffn_w1"], gate_up[:, :D], gate_up[:, D:], *a["L0_ffn_w2"], a["L0_ffn_shared_down"]]
    slots += [*out_slices(a["L0_attn_w_out"]), *out_slices(a["L0_xattn_o_w"])]
    consts = constants()
    q_b, k_b = a["L0_xattn_q_b"].reshape(D, 1), a["L0_xattn_k_b"].reshape(D, 1)
    row_consts = np.stack([np.broadcast_to(a["L0_xattn_v_b"], (P, D)), np.broadcast_to(a["L0_xattn_o_b"], (P, D)),
                           consts.pop("rope")], axis=1)
    arrays = dict(
        x=np.ascontiguousarray(x.transpose(0, 2, 1, 3)), x_t=group_t(a["x"]), ctx_t=group_t(a["ctx_1024"]),
        weights=np.ascontiguousarray(np.stack(slots, axis=1)),
        router=np.concatenate([a["L0_ffn_router_w"], a["L0_ffn_shared_gate_w"]], axis=1),
        row_consts=row_consts,
        biases=np.concatenate([q_b, swap_halves(q_b), k_b, swap_halves(k_b)], axis=1), **consts)

    nc = bacc.Bacc("TRN2", target_bir_lowering=False, num_devices=1)
    aps = {k: nc.dram_tensor("in_" + k, v.shape, mybir.dt.from_np(v.dtype), kind="ExternalInput").ap()
           for k, v in arrays.items()}
    out = nc.dram_tensor("out", (NG, P, TILES, D), F32, kind="ExternalOutput").ap()
    decoder_layer(nc, out=out, **aps)
    result = run_bass_kernel_spmd(nc, [{"in_" + k: v for k, v in arrays.items()}], core_ids=[0])
    got = result.results[0]["out"]
    return np.ascontiguousarray(got.transpose(0, 2, 1, 3)).reshape(S, S, D)
```

```python
from contextlib import ExitStack

import numpy as np

import concourse.bass as bass
from concourse import mybir

ALU = mybir.AluOpType
ACT = mybir.ActivationFunctionType
F32 = mybir.dt.float32
F16 = mybir.dt.float16
BF16 = mybir.dt.bfloat16
AX_X = mybir.AxisListType.X

P = 128
D = 128
H, DH, S = 16, 8, 64
TOKENS = 64 * S
TILES = 4
G = TILES * P
NG = TOKENS // G
E = 8
PAIRS = H // 2
BANKS = 8
MASKED = -1.0e30
EPS = 1e-5
SCALE = float(DH) ** -0.5
W_SCALE = 256.0
INV_SCALE = 64.0

W_QA, W_KA, W_VA, W_QB, W_QBR, W_KB, W_KBR, W_VB = range(8)
W_1 = 8
W_UP = W_1 + E + 1
W_2 = W_UP + 1
SHARED = E - 1
W_OA = W_2 + E + 1
W_OB = W_OA + 4
NW = W_OB + 4
NW16 = W_UP + 1

ROUTER = 16
ROWS, BLOCKS = 16 * 3, 16 * 12
STACK = ROWS + BLOCKS
N_LOADS = 9
ZERO_FILLS = 5


def decoder_layer(nc, x, x_t, ctx_t, weights, router, row_consts, v_biases, biases, c_ident, c_masks,
                  c_den_ones, c_spread, c_own_head, out):
    ctx = ExitStack()
    with ctx:
        def sb(name, shape, dt=F32):
            return ctx.enter_context(nc.sbuf_tensor(name, shape, dt))

        def sem(name):
            return ctx.enter_context(nc.semaphore(name))

        w = sb("w", [P, NW, D])
        w16 = sb("w16", [P, 2, NW16, D], F16)
        rw = sb("rw", [P, E + 1])
        rw16 = sb("rw16", [P, 2, E + 1], F16)
        rows3 = sb("rows3", [P, 2, D])
        v_bias = sb("v_bias", [P, 2, P])
        out_bias = sb("out_bias", [P, 1, D])
        bias = sb("bias", [P, 4])
        bias_s = sb("bias_s", [P, 4])
        ident = sb("ident", [P, P])
        masks = sb("masks", [P, 4, S], BF16)
        den_ones = sb("den_ones", [P, 8, 32])
        spread = sb("spread", [P, 8, P], F16)
        own_head = sb("own_head", [P, P])
        half_neg = sb("half_neg", [P, TILES])
        warm = sb("warm", [P, 4])
        seg = sb("seg", [P, TILES, E])
        xt = sb("xt", [P, G])
        ct = sb("ct", [P, G])
        xn = sb("xn", [P, TILES, D])
        xt16, ct16 = sb("xt16", [P, 2, G], F16), sb("ct16", [P, 2, G], F16)
        split = {n: sb("split_" + n, [P, 2, G], F16) for n in ("qA", "kA", "qB", "kB")}
        q_rows = {a: sb("q_rows" + a, [P, 4, G], F16) for a in "AB"}
        k_rows = {a: sb("k_rows" + a, [P, 4, G], F16) for a in "AB"}
        q_block = {a: sb("q_block" + a, [P, 4, 4, G], F16) for a in "AB"}
        k_block = {a: sb("k_block" + a, [P, 4, 4, G], F16) for a in "AB"}
        v_block = {a: sb("v_block" + a, [P, TILES, PAIRS, 32]) for a in "AB"}
        neg_max = {a: sb("neg_max" + a, [P, TILES, H]) for a in "AB"}
        neg_max_t = {a: sb("neg_max_t" + a, [H, G], F16) for a in "AB"}
        probs = sb("probs", [P, 2, H * S])
        ctx_raw = {a: sb("ctx_raw" + a, [P, TILES, 256]) for a in "AB"}
        inv_den = sb("inv_den", [P, P])
        inv_own = sb("inv_own", [P, P])
        inv_hi, inv_lo = sb("inv_hi", [P, P], F16), sb("inv_lo", [P, P], F16)
        ctx_n = sb("ctx_n", [P, TILES, 2, 2, S])
        ctx_s = sb("ctx_s", [P, TILES, 2, S])
        roped = sb("roped", [P, 2, G])
        rope_sum = sb("rope_sum", [P, G])
        res = sb("res", [P, TILES, D])
        stats = sb("stats", [P, TILES, 6])
        mean_var = sb("mean_var", [P, TILES, 2])
        rstd = sb("rstd", [P, TILES])
        veps = sb("veps", [P, TILES])
        eps = sb("eps", [P, TILES])
        x1 = sb("x1", [P, TILES, D])
        x1b = sb("x1b", [P, TILES, D])
        x1t16 = sb("x1t16", [P, 2, G], F16)
        x2 = sb("x2", [P, TILES, D])
        x2t16 = sb("x2t16", [P, 2, G], F16)
        x3 = sb("x3", [P, TILES, D])
        logit = sb("logit", [P, TILES, E + 1])
        top = sb("top", [P, TILES, 8])
        small = [sb(f"small{k}", [P, TILES, E]) for k in range(6)]
        col = [sb(f"col{k}", [P, TILES]) for k in range(4)]
        gate = sb("gate", [P, TILES, E + 1])
        act_h = sb("act_h", [P, 2, G])
        sh_h = sb("sh_h", [P, G])
        moe_sum = sb("moe_sum", [P, TILES, D])
        moe_total = sb("moe_total", [P, TILES, D])

        bank = [ctx.enter_context(nc.psum_tensor(f"bank{i}", [P, 512], F32)) for i in range(BANKS)]
        scratch = {a: nc.dram_tensor("split_" + a, [4, P, G], F16).ap() for a in "AB"}

        score_bank, t_bank = bank[0:2], bank[2:4]
        ctx_bank, y_bank, den_bank, side_bank = bank[4], bank[5], bank[6], bank[7]
        expert_bank = bank[4:6]

        def per_attention(name):
            return {a: sem(name + a) for a in "AB"}

        loaded, pool_const = sem("weights_loaded"), sem("pool_const")
        zeroed = per_attention("zeroed")
        carried = sem("waits_carried")
        warm_written = sem("warm_written")
        w_hi_ready, w_split = sem("w_hi_ready"), sem("w_split")
        bias_scaled, v_bias_projected, out_bias_ready = (sem("bias_scaled"), sem("v_bias_projected"),
                                                         sem("out_bias_ready"))
        xt_hi, xt_split, ct_hi, ct_split = sem("xt_hi"), sem("xt_split"), sem("ct_hi"), sem("ct_split")
        x_hi = per_attention("x_hi")
        first_in, experts_in = sem("first_in"), sem("experts_in")
        xt_in, ct_in, xn_in, stored = sem("xt_in"), sem("ct_in"), sem("xn_in"), sem("stored")
        q_written, k_written = per_attention("q_written"), per_attention("k_written")
        v_written, v_placed = per_attention("v_written"), per_attention("v_placed")
        hi_ready, split_ready = per_attention("hi_ready"), per_attention("split_ready")
        spilled = per_attention("spilled")
        scores_stacked, t_stacked = per_attention("scores_stacked"), per_attention("t_stacked")
        roped_ready, rope_sum_ready = sem("roped_ready"), sem("rope_sum_ready")
        scores_written, max_ready = per_attention("scores_written"), per_attention("max_ready")
        max_turned, max_t_ready = per_attention("max_turned"), per_attention("max_t_ready")
        max_stacked = per_attention("max_stacked")
        t_written, probs_ready = per_attention("t_written"), per_attention("probs_ready")
        probs_used = per_attention("probs_used")
        ctx_written, ctx_kept = per_attention("ctx_written"), per_attention("ctx_kept")
        inv_step, inv_ready = per_attention("inv_step"), per_attention("inv_ready")
        spread_written, ctx_n_ready = per_attention("spread_written"), per_attention("ctx_n_ready")
        ctx_s_ready = per_attention("ctx_s_ready")
        y_written, x_turned, xt_ready = (per_attention("y_written"), per_attention("x_turned"),
                                         per_attention("xt_ready"))
        norms = "ABC"
        res_ready, rstd_ready, normed = ({a: sem(name + a) for a in norms}
                                         for name in ("res_ready", "rstd_ready", "normed"))
        stats_ready, var_ready = ({a: sem(name + a) for a in norms} for name in ("stats_ready", "var_ready"))
        veps_ready = {a: sem("veps_ready" + a) for a in norms}
        biased = sem("biased")
        logits_written, logit_ready, exp_ready = sem("logits_written"), sem("logit_ready"), sem("exp_ready")
        router_step, gates_ready = sem("router_step"), sem("gates_ready")
        h_written, silu_ready = sem("h_written"), sem("silu_ready")
        up_written, sh_ready = sem("up_written"), sem("sh_ready")
        expert_written, expert_added = sem("expert_written"), sem("expert_added")

        def bank_of(e):
            return (e + 1) % 2 if e < 6 else e % 2

        block = ctx.enter_context(nc.Block())

        def steps(step, eng):
            step(0, a=True, b=False, c=False, d=False, nxt=True)
            step(1, a=True, b=True, c=False, d=False, nxt=True)
            step(2, a=True, b=True, c=True, d=False, nxt=True)
            with eng.Fori(3, NG - 1) as n:
                step(n, a=True, b=True, c=True, d=True, nxt=True)
            step(NG - 1, a=True, b=True, c=True, d=True, nxt=False)
            step(NG, a=False, b=True, c=True, d=True, nxt=False)
            step(NG + 1, a=False, b=False, c=True, d=True, nxt=False)
            step(NG + 2, a=False, b=False, c=False, d=True, nxt=False)

        @block.sync
        def _(sp):
            sp.dma_start(xt[:], x_t[0]).then_inc(first_in, 16)
            sp.dma_start(w[:, 0:W_QB], weights[:, 0:W_QB]).then_inc(first_in, 16)
            sp.dma_start(ident[:], c_ident).then_inc(first_in, 16)

            def other_loads():
                sp.dma_start(w[:, W_QB:W_1], weights[:, W_QB:W_1]).then_inc(loaded, 16)
                sp.dma_start(w[:, W_OA:NW], weights[:, W_OA:NW]).then_inc(loaded, 16)
                for dst, src in ((rows3, row_consts), (v_bias, v_biases), (bias, biases), (masks, c_masks), (den_ones, c_den_ones),
                                 (spread, c_spread), (own_head, c_own_head)):
                    sp.dma_start(dst[:], src).then_inc(loaded, 16)
                sp.dma_start(ct[:], ctx_t[0]).then_inc(ct_in, 16)
                sp.dma_start(xn[:], x[0]).then_inc(xn_in, 16)

            def expert_loads():
                sp.dma_start(rw[:], router).then_inc(experts_in, 16)
                sp.dma_start(w[:, W_1:W_OA], weights[:, W_1:W_OA]).then_inc(experts_in, 16)

            def carry(n):
                if not isinstance(n, int):
                    sp.sem_inc(carried, 1)

            def stack_rows(a, part):
                base, order, rows, done = ((0, (0, 0, 1), q_rows, scores_stacked) if part == "q" else
                                           (2, (0, 1, 0), k_rows, t_stacked))
                for s, hl in enumerate(order):
                    src = scratch[a][base + hl].rearrange("(g r) t -> r g t", g=4)
                    sp.dma_start(rows[a][32 * s:32 * s + 32], src).then_inc(done[a], 16)

            def stack_blocks(a, part):
                base, order, blocks, done = ((0, (0, 0, 1), q_block, t_stacked) if part == "q" else
                                             (2, (0, 1, 0), k_block, scores_stacked))
                for s, hl in enumerate(order):
                    src = scratch[a][base + hl].rearrange("(g r) t -> r g t", g=4)
                    for r in range(4):
                        sp.dma_start(blocks[a][32 * s + 8 * r:32 * s + 8 * r + 8, :, r, :],
                                     src[8 * r:8 * r + 8]).then_inc(done[a], 16)

            def spill(a, part):
                base = 0 if part == "q" else 2
                sp.dma_start(scratch[a][base:base + 2].rearrange("s p t -> p s t"),
                             split[part + a][:]).then_inc(spilled[a], 16)

            def maxima(a):
                for r in range(4):
                    sp.dma_start(q_block[a][96 + r:97 + r, :, r, :],
                                 neg_max_t[a][4 * r:4 * r + 4]).then_inc(max_stacked[a], 16)

            def step(n, a, b, c, d, nxt):
                m = n - 1
                if a:
                    sp.wait_ge(max_t_ready["A"], n + 1)
                    carry(n)
                    maxima("A")
                if nxt:
                    sp.wait_ge(scores_stacked["A"], STACK * n + STACK)
                    carry(n)
                    sp.wait_ge(t_stacked["A"], STACK * n + STACK)
                    carry(n)
                    sp.wait_ge(split_ready["A"], 2 * n + 3)
                    carry(n)
                    spill("A", "q")
                    sp.wait_ge(split_ready["A"], 2 * n + 4)
                    carry(n)
                    spill("A", "k")
                if nxt:
                    sp.wait_ge(xt_split, n + 2)
                    carry(n)
                    sp.dma_start(xt[:], x_t[n + 2]).then_inc(xt_in, 16)
                if b:
                    sp.wait_ge(max_t_ready["B"], m + 1)
                    carry(n)
                    maxima("B")
                if nxt:
                    sp.wait_ge(spilled["A"], 32 * n + 64)
                    carry(n)
                    stack_rows("A", "q")
                    stack_blocks("A", "k")
                if d:
                    sp.wait_ge(normed["C"], n - 2)
                    carry(n)
                    sp.dma_start(out[n - 3], x3[:]).then_inc(stored, 16)
                if nxt:
                    sp.wait_ge(t_written["A"], 8 * n + 8)
                    carry(n)
                    stack_rows("A", "k")
                    stack_blocks("A", "q")
                if a:
                    sp.wait_ge(split_ready["B"], 2 * n + 1)
                    carry(n)
                    if b:
                        sp.wait_ge(scores_stacked["B"], STACK * n)
                        carry(n)
                        sp.wait_ge(t_stacked["B"], STACK * n)
                        carry(n)
                    spill("B", "k")
                    sp.wait_ge(spilled["B"], 32 * n + 16)
                    carry(n)
                    stack_blocks("B", "k")
                    if b:
                        sp.wait_ge(t_written["B"], 8 * m + 8)
                        carry(n)
                    stack_rows("B", "k")
                if nxt:
                    sp.wait_ge(res_ready["A"], n + 1)
                    carry(n)
                    sp.dma_start(xn[:], x[n + 1]).then_inc(xn_in, 16)
                    sp.wait_ge(ct_split, n + 1)
                    carry(n)
                    sp.dma_start(ct[:], ctx_t[n + 1]).then_inc(ct_in, 16)
                if a:
                    sp.wait_ge(split_ready["B"], 2 * n + 2)
                    carry(n)
                    spill("B", "q")
                    sp.wait_ge(spilled["B"], 32 * n + 32)
                    carry(n)
                    stack_rows("B", "q")
                    stack_blocks("B", "q")

            other_loads()
            sp.wait_ge(split_ready["A"], 1)
            spill("A", "q")
            sp.wait_ge(split_ready["A"], 2)
            spill("A", "k")
            sp.wait_ge(zeroed["A"], ZERO_FILLS)
            sp.wait_ge(spilled["A"], 32)
            stack_rows("A", "q")
            stack_blocks("A", "k")
            sp.wait_ge(xt_split, 1)
            sp.dma_start(xt[:], x_t[1]).then_inc(xt_in, 16)
            expert_loads()
            stack_rows("A", "k")
            stack_blocks("A", "q")
            sp.wait_ge(zeroed["B"], ZERO_FILLS)
            sp.sem_inc(stored, 16)
            steps(step, sp)
            sp.wait_ge(xt_in, 16 * NG)
            sp.wait_ge(stored, 16 * NG + 16)

        @block.gpsimd
        def _(pool):
            pool.memset(v_block["A"][:], 0.0).then_inc(zeroed["A"], 1)
            pool.memset(q_block["A"][:], 0.0).then_inc(zeroed["A"], 1)
            pool.memset(half_neg[:], -0.5).then_inc(pool_const, 1)
            pool.memset(eps[:], EPS).then_inc(pool_const, 1)
            pool.memset(seg[:], 1.0).then_inc(pool_const, 1)
            pool.wait_ge(pool_const, 3)
            pool.memset(seg[:, :, 0:1], 0.0).then_inc(pool_const, 1)
            pool.memset(q_block["B"][:], 0.0).then_inc(zeroed["B"], 1)
            pool.memset(v_block["B"][:], 0.0).then_inc(zeroed["B"], 1)
            pool.wait_ge(xt_hi, 2)
            pool.tensor_tensor(xt16[:, 1, :], xt[:], xt16[:, 0, :], ALU.subtract).then_inc(xt_split, 1)

            def rope_sum_and_lo(n, part, k):
                pool.wait_ge(roped_ready, 4 * n + 2 * k)
                pool.tensor_tensor(rope_sum[:], roped[:, 0, :], roped[:, 1, :], ALU.add)\
                    .then_inc(rope_sum_ready, 1)
                pool.wait_ge(rope_sum_ready, 2 * n + k)
                pool.wait_ge(hi_ready["B"], 2 * n + k)
                pool.tensor_tensor(split[part + "B"][:, 1, :], rope_sum[:], split[part + "B"][:, 0, :],
                                   ALU.subtract).then_inc(split_ready["B"], 1)

            def inverse_root(n, j):
                pool.wait_ge(var_ready[j], 4 * n + 4)
                pool.tensor_tensor(veps[:], mean_var[:, :, 1], eps[:], ALU.add).then_inc(veps_ready[j], 1)
                pool.wait_ge(veps_ready[j], n + 1)
                pool.tensor_tensor(rstd[:], veps[:], half_neg[:], ALU.pow).then_inc(rstd_ready[j], 1)

            def bias_residual(n):
                pool.wait_ge(out_bias_ready, 1)
                pool.wait_ge(normed["A"], n + 1)
                pool.tensor_tensor(x1b[:], x1[:], out_bias[:].to_broadcast([P, TILES, D]), ALU.add)\
                    .then_inc(biased, 1)

            def step(n, a, b, c, d, nxt):
                m, k = n - 1, n - 2
                if a:
                    pool.wait_ge(ct_hi, n + 1)
                    pool.tensor_tensor(ct16[:, 1, :], ct[:], ct16[:, 0, :], ALU.subtract).then_inc(ct_split, 1)
                if not b and not c:
                    pool.wait_ge(loaded, 16 * N_LOADS)
                if d:
                    inverse_root(n - 3, "C")
                if a:
                    rope_sum_and_lo(n, "k", 1)
                    inverse_root(n, "A")
                    rope_sum_and_lo(n, "q", 2)
                if b:
                    inverse_root(m, "B")
                    pool.wait_ge(res_ready["B"], m + 1)
                if a:
                    bias_residual(n)
                if nxt:
                    pool.wait_ge(xt_hi, n + 3)
                    pool.tensor_tensor(xt16[:, 1, :], xt[:], xt16[:, 0, :], ALU.subtract).then_inc(xt_split, 1)

            steps(step, pool)

        @block.tensor
        def _(pe):
            def three_products(dst, weights16, slot, moving16):
                pe.matmul(dst, weights16[:, 0, slot, :], moving16[:, 0, :], start=True, stop=False)
                pe.matmul(dst, weights16[:, 0, slot, :], moving16[:, 1, :], start=False, stop=False)
                return pe.matmul(dst, weights16[:, 1, slot, :], moving16[:, 0, :], start=False, stop=True)

            def project(slot, moving):
                return three_products(side_bank[:, :], w16, slot, moving)

            def project_rows(dst, source16, moving16):
                width = moving16[0].shape[-1]
                for t in range(TILES):
                    tokens = slice(t * P, (t + 1) * P)
                    out = dst[:, t * width:(t + 1) * width]
                    pe.matmul(out, source16[:, 0, tokens], moving16[0], start=True, stop=False)
                    pe.matmul(out, source16[:, 0, tokens], moving16[1], start=False, stop=False)
                    mm = pe.matmul(out, source16[:, 1, tokens], moving16[0], start=False, stop=True)
                return mm

            def project_v(slot, source16):
                return project_rows(side_bank, source16, (w16[:, 0, slot, :], w16[:, 1, slot, :]))

            def turn(dst, source):
                for t in range(TILES):
                    mm = pe.transpose(dst[:, t * P:(t + 1) * P], source(t), ident[:])
                return mm

            def half_scores(dst, t, half, a, rows, blocks, mask):
                if a == "B":
                    pe.matmul(dst[:, :].rearrange("p (h k) -> p h k", k=S),
                              masks[:, 0:2, :].rearrange("p b q -> p (b q)"),
                              mask.unsqueeze(1).to_broadcast([P, 8, S]),
                              start=True, stop=False, skip_group_check=True)
                for gg in range(2):
                    g = 2 * half + gg
                    for b in range(2):
                        lo = t * P + 64 * b
                        mm = pe.matmul(dst[64 * b:64 * b + 64, gg * 256:gg * 256 + 256],
                                       rows[a][:, g, lo:lo + 64], blocks[a][:, g, :, lo:lo + 64],
                                       start=(a == "A"), stop=True, skip_group_check=True)
                return mm

            def scores(n, a, t):
                for half in range(2):
                    if t > 0:
                        pe.wait_ge(max_ready[a], 8 * n + 2 * t + half - 1)
                    half_scores(score_bank[half], t, half, a, q_rows, k_block, masks[:, 2, :])\
                        .then_inc(scores_written[a], 1)

            def turn_maxima(n, a):
                pe.wait_ge(max_ready[a], 8 * n + 8)
                for t in range(TILES):
                    mm = pe.transpose(side_bank[0:H, t * P:(t + 1) * P], neg_max[a][:, t, :], ident[:])
                mm.then_inc(max_turned[a], 1)

            def t_scores(n, a, t):
                if t == 0:
                    pe.wait_ge(max_stacked[a], 64 * n + 64)
                for half in range(2):
                    if t > 0:
                        pe.wait_ge(probs_ready[a], 8 * n + 2 * t + half - 1)
                    half_scores(t_bank[half], t, half, a, k_rows, q_block, masks[:, 3, :])\
                        .then_inc(t_written[a], 1)

            def context(n, a, t):
                for i in range(2):
                    pe.wait_ge(probs_ready[a], 8 * n + 2 * t + i + 1)
                    if t == 2 and i == 0:
                        pe.wait_ge(ctx_kept[a], 2 * n + 1)
                    pairs = range(4 * i, 4 * i + 4)
                    for p in pairs:
                        c, at = p % 4, (t % 2) * 256 + i * P
                        mo = pe.matmul(ctx_bank[32 * c:32 * c + 32, at:at + P], v_block[a][:, t, p, :],
                                       probs[:, t % 2, p * P:(p + 1) * P], start=True, stop=True,
                                       skip_group_check=True)
                    if t % 2 == 1 and i == 1:
                        mo.then_inc(ctx_written[a], 1)
                    for p in pairs:
                        c = p % 4
                        md = pe.matmul(den_bank[32 * c:32 * c + 32, 0:P], den_ones[:, 2 * t + i, :],
                                       probs[:, t % 2, p * P:(p + 1) * P], start=(t == 0 and i == 0),
                                       stop=(t == TILES - 1 and i == 1), skip_group_check=True)
                md.then_inc(probs_used[a], 1)

            def spread_sums(n, a, u):
                if u == 0:
                    pe.wait_ge(inv_ready[a], 2 * n + 2)
                else:
                    pe.wait_ge(ctx_n_ready[a], 2 * n + 1)
                for k in range(4):
                    for part in (inv_hi, inv_lo):
                        mm = pe.matmul(y_bank[:, k * P:(k + 1) * P], spread[:, 4 * u + k, :], part[:],
                                       start=(part is inv_hi), stop=(part is inv_lo))
                mm.then_inc(spread_written[a], 1)

            def out_project(n, a, slot):
                pe.wait_ge(ctx_s_ready[a], 2 * n + 2)
                for t in range(TILES):
                    for i in range(2):
                        for b in range(2):
                            mm = pe.matmul(y_bank[64 * b:64 * b + 64, t * P:(t + 1) * P],
                                           ctx_s[:, t, i, :], w[:, slot + 2 * i + b, :],
                                           start=(i == 0), stop=(i == 1), skip_group_check=True)
                mm.then_inc(y_written[a], 1)

            def expert(n, e):
                if e != SHARED:
                    pe.wait_ge(silu_ready, (E + 1) * n + e + 1)
                    source = act_h[:, e % 2, :]
                else:
                    pe.wait_ge(sh_ready, n + 1)
                    source = sh_h[:]
                if e == 0:
                    pe.wait_ge(res_ready["B"], n + 1)
                elif e == 1:
                    pe.wait_ge(ctx_kept["B"], 2 * n + 2)
                    if not isinstance(n, int) or n > 0:
                        pe.wait_ge(expert_added, (E + 1) * n)
                elif e == 6:
                    pe.wait_ge(expert_added, (E + 1) * n + 6)
                else:
                    pe.wait_ge(expert_added, (E + 1) * n + e - 1)
                out_bank = expert_bank[bank_of(e)]
                for t in range(TILES):
                    mm = pe.matmul(out_bank[:, t * P:(t + 1) * P], source[:, t * P:(t + 1) * P],
                                   w[:, W_2 + e, :], start=True, stop=True)
                mm.then_inc(expert_written, 1)

            def hidden(n, e):
                if e >= 2:
                    pe.wait_ge(silu_ready, (E + 1) * n + e - 1)
                three_products(t_bank[e % 2][:, :], w16, W_1 + e, x2t16).then_inc(h_written, 1)

            def up(n):
                pe.wait_ge(silu_ready, (E + 1) * n + E)
                three_products(t_bank[1][:, :], w16, W_UP, x2t16).then_inc(up_written, 1)

            def step(n, a, b, c, d, nxt):
                m, k = n - 1, n - 2
                if c:
                    expert(k, 0)
                    hidden(k, 2)
                    expert(k, 1)
                    hidden(k, 3)
                if a and b:
                    pe.wait_ge(v_placed["A"], 2 * n + 2)
                    turn_maxima(n, "A")
                if b:
                    pe.wait_ge(scores_stacked["B"], STACK * m + STACK)
                    if a:
                        pe.wait_ge(max_ready["A"], 8 * n + 8)
                    scores(m, "B", 0)
                if nxt:
                    pe.wait_ge(xt_split, n + 2)
                    pe.wait_ge(max_t_ready["A"], n + 1)
                    project(W_QA, xt16).then_inc(q_written["A"], 1)
                if b:
                    scores(m, "B", 1)
                if c:
                    expert(k, 2)
                    hidden(k, 4)
                if nxt:
                    pe.wait_ge(split_ready["A"], 2 * n + 3)
                    project(W_KA, xt16).then_inc(k_written["A"], 1)
                if b:
                    scores(m, "B", 2)
                if c:
                    expert(k, 3)
                    hidden(k, 5)
                if b:
                    scores(m, "B", 3)
                if c:
                    expert(k, 4)
                    expert(k, 5)
                if a:
                    if c:
                        pe.wait_ge(silu_ready, (E + 1) * k + 6)
                    pe.wait_ge(t_stacked["A"], STACK * n + STACK)
                    t_scores(n, "A", 0)
                if b:
                    if nxt:
                        pe.wait_ge(split_ready["A"], 2 * n + 4)
                    elif a:
                        pe.wait_ge(max_t_ready["A"], n + 1)
                    turn_maxima(m, "B")
                if a:
                    t_scores(n, "A", 1)
                    pe.wait_ge(v_placed["A"], 2 * n + 2)
                    if c:
                        pe.wait_ge(expert_added, (E + 1) * k + 6)
                    context(n, "A", 0)
                    t_scores(n, "A", 2)
                    context(n, "A", 1)
                    t_scores(n, "A", 3)
                    if b:
                        pe.wait_ge(max_t_ready["B"], m + 1)
                    elif nxt:
                        pe.wait_ge(split_ready["A"], 2 * n + 4)
                    pe.wait_ge(ct_split, n + 1)
                    project(W_KB, ct16).then_inc(k_written["B"], 1)
                    context(n, "A", 2)
                if b:
                    if a:
                        pe.wait_ge(probs_ready["A"], 8 * n + 8)
                    elif c:
                        pe.wait_ge(expert_added, (E + 1) * k + 6)
                    pe.wait_ge(t_stacked["B"], STACK * m + STACK)
                    t_scores(m, "B", 0)
                if a:
                    context(n, "A", 3)
                    pe.wait_ge(roped_ready, 4 * n + 1)
                    project(W_KBR, ct16).then_inc(k_written["B"], 1)
                if b:
                    t_scores(m, "B", 1)
                    if a:
                        pe.wait_ge(ctx_kept["A"], 2 * n + 2)
                        pe.wait_ge(inv_step["A"], 2 * n + 1)
                    context(m, "B", 0)
                if a:
                    if not b:
                        pe.wait_ge(out_bias_ready, 1)
                    spread_sums(n, "A", 0)
                if b:
                    t_scores(m, "B", 2)
                    context(m, "B", 1)
                if a:
                    spread_sums(n, "A", 1)
                if nxt:
                    pe.wait_ge(scores_stacked["A"], STACK * n + 2 * STACK)
                    if b:
                        pe.wait_ge(max_ready["B"], 8 * m + 8)
                    else:
                        pe.wait_ge(max_ready["A"], 8 * n + 8)
                    scores(n + 1, "A", 0)
                if b:
                    t_scores(m, "B", 3)
                if nxt:
                    scores(n + 1, "A", 1)
                if b:
                    context(m, "B", 2)
                if nxt:
                    scores(n + 1, "A", 2)
                if a:
                    out_project(n, "A", W_OA)
                if nxt:
                    scores(n + 1, "A", 3)
                if b:
                    context(m, "B", 3)
                if a:
                    pe.wait_ge(roped_ready, 4 * n + 2)
                    project_v(W_VB, ct16).then_inc(v_written["B"], 1)
                if c:
                    if b:
                        pe.wait_ge(probs_ready["B"], 8 * m + 8)
                    hidden(k, 6)
                    hidden(k, 7)
                    if b:
                        pe.wait_ge(ctx_kept["B"], 2 * m + 2)
                    expert(k, 6)
                if b:
                    if a:
                        pe.wait_ge(res_ready["A"], n + 1)
                    spread_sums(m, "B", 0)
                if a:
                    pe.wait_ge(normed["A"], n + 1)
                    turn(den_bank, lambda t: x1[:, t, :]).then_inc(x_turned["A"], 1)
                if c:
                    hidden(k, 8)
                if b:
                    spread_sums(m, "B", 1)
                if a:
                    pe.wait_ge(v_placed["B"], 2 * n + 2)
                    pe.wait_ge(xt_ready["A"], n + 1)
                    project(W_QB, x1t16).then_inc(q_written["B"], 1)
                if c:
                    up(k)
                if a:
                    pe.wait_ge(roped_ready, 4 * n + 3)
                    project(W_QBR, x1t16).then_inc(q_written["B"], 1)
                if b:
                    out_project(m, "B", W_OB)
                if nxt:
                    pe.wait_ge(roped_ready, 4 * n + 4)
                    project_v(W_VA, xt16).then_inc(v_written["A"], 1)
                if c:
                    if b:
                        pe.wait_ge(res_ready["B"], m + 1)
                    expert(k, SHARED)
                if b:
                    pe.wait_ge(normed["B"], m + 1)
                    turn(t_bank[1], lambda t: x2[:, t, :]).then_inc(x_turned["B"], 1)
                if c:
                    expert(k, 8)
                if b:
                    if not c:
                        pe.wait_ge(w_split, 4)
                    pe.wait_ge(xt_ready["B"], m + 1)
                    project_rows(den_bank, x2t16, (rw16[:, 0, :], rw16[:, 1, :])).then_inc(logits_written, 1)
                    hidden(m, 0)
                    hidden(m, 1)
                if c:
                    pe.wait_ge(expert_added, (E + 1) * k + E)

            pe.wait_ge(first_in, 48)
            pe.wait_ge(w_split, 1)
            pe.wait_ge(xt_split, 1)
            project(W_QA, xt16).then_inc(q_written["A"], 1)
            pe.wait_ge(split_ready["A"], 1)
            project(W_KA, xt16).then_inc(k_written["A"], 1)
            pe.wait_ge(split_ready["A"], 2)
            project_v(W_VA, xt16).then_inc(v_written["A"], 1)
            pe.wait_ge(v_placed["A"], 2)
            pe.wait_ge(zeroed["A"], ZERO_FILLS)
            pe.wait_ge(scores_stacked["A"], STACK)
            for t in range(TILES):
                scores(0, "A", t)
            turn_maxima(0, "A")
            pe.wait_ge(zeroed["B"], ZERO_FILLS)
            pe.wait_ge(loaded, 16 * N_LOADS)
            for i in range(2):
                mm = pe.matmul(y_bank[:, 0:D], v_bias[:, i, :], w[:, W_OB + 2 * i, :],
                               start=(i == 0), stop=(i == 1))
            mm.then_inc(v_bias_projected, 1)
            pe.wait_ge(w_split, 2)
            steps(step, pe)

        @block.scalar
        def _(act):
            def hi_part(part):
                act.activation(split[part + "A"][:, 0, :], side_bank[:, :], ACT.Copy, scale=1 / W_SCALE)\
                   .then_inc(hi_ready["A"], 1)

            def place_v(a):
                for b in range(2):
                    act.activation(v_block[a][64 * b:64 * b + 64, :, :, 16 * b:16 * b + 16],
                                   side_bank[64 * b:64 * b + 64, :].rearrange("p (t c d) -> p t c d",
                                                                              t=TILES, d=16),
                                   ACT.Copy, scale=1 / W_SCALE).then_inc(v_placed[a], 1)

            def maxima(a):
                act.copy(neg_max_t[a][:], side_bank[0:H, :]).then_inc(max_t_ready[a], 1)

            def exps(n, a, t):
                for half in range(2):
                    act.wait_ge(t_written[a], 8 * n + 2 * t + half + 1)
                    act.activation(probs[:, t % 2, half * 512:half * 512 + 512], t_bank[half][:, :],
                                   ACT.Exp, scale=SCALE).then_inc(probs_ready[a], 1)

            def keep_context(n, a, u):
                act.wait_ge(ctx_written[a], 2 * n + u + 1)
                act.copy(ctx_raw[a][:, 2 * u:2 * u + 2, :].rearrange("p t c -> p (t c)"), ctx_bank[:, :])\
                   .then_inc(ctx_kept[a], 1)

            def load_table(function, at):
                act.activation(warm[:, at:at + 1], half_neg[:, 0:1], function).then_inc(warm_written, 1)

            def silu(n, e):
                act.wait_ge(h_written, (E + 1) * n + e + 1)
                if e >= 2:
                    act.wait_ge(expert_written, (E + 1) * n + e - 1)
                act.activation(act_h[:, e % 2, :], t_bank[e % 2][:, :], ACT.Silu,
                               scale=1 / W_SCALE).then_inc(silu_ready, 1)

            def step(n, a, b, c, d, nxt):
                m, k = n - 1, n - 2
                if c:
                    silu(k, 2)
                    silu(k, 3)
                if a and b:
                    act.wait_ge(max_turned["A"], n + 1)
                    maxima("A")
                if nxt:
                    act.wait_ge(spilled["A"], 32 * n + 32)
                    act.wait_ge(q_written["A"], n + 2)
                    hi_part("q")
                if a:
                    act.wait_ge(ct_in, 16 * n + 16)
                    if b:
                        act.wait_ge(v_written["B"], n)
                    act.copy(ct16[:, 0, :], ct[:]).then_inc(ct_hi, 1)
                if c:
                    silu(k, 4)
                if nxt:
                    act.wait_ge(k_written["A"], n + 2)
                    hi_part("k")
                if c:
                    silu(k, 5)
                    load_table(ACT.Exp, 0)
                if a:
                    exps(n, "A", 0)
                if b:
                    act.wait_ge(max_turned["B"], m + 1)
                    maxima("B")
                if a:
                    exps(n, "A", 1)
                    act.wait_ge(probs_used["A"], 4 * n + 1)
                    exps(n, "A", 2)
                    keep_context(n, "A", 0)
                    act.wait_ge(probs_used["A"], 4 * n + 2)
                    exps(n, "A", 3)
                if b:
                    if a:
                        act.wait_ge(probs_used["A"], 4 * n + 3)
                    exps(m, "B", 0)
                if a:
                    keep_context(n, "A", 1)
                if b:
                    if a:
                        act.wait_ge(probs_used["A"], 4 * n + 4)
                    exps(m, "B", 1)
                if b:
                    act.wait_ge(probs_used["B"], 4 * m + 1)
                    exps(m, "B", 2)
                if a:
                    act.wait_ge(rope_sum_ready, 2 * n + 1)
                    if b:
                        act.wait_ge(spilled["B"], 32 * n)
                    act.copy(split["kB"][:, 0, :], rope_sum[:]).then_inc(hi_ready["B"], 1)
                if b:
                    keep_context(m, "B", 0)
                    act.wait_ge(probs_used["B"], 4 * m + 2)
                    exps(m, "B", 3)
                    if c:
                        load_table(ACT.Silu, 1)
                    keep_context(m, "B", 1)
                if c:
                    silu(k, 6)
                    silu(k, 7)
                if a:
                    act.wait_ge(x_turned["A"], n + 1)
                    act.copy(x1t16[:, 0, :], den_bank[:, :]).then_inc(x_hi["A"], 1)
                    act.wait_ge(v_written["B"], n + 1)
                    place_v("B")
                if c:
                    silu(k, 8)
                if a:
                    act.wait_ge(rope_sum_ready, 2 * n + 2)
                    act.copy(split["qB"][:, 0, :], rope_sum[:]).then_inc(hi_ready["B"], 1)
                if nxt:
                    act.wait_ge(v_written["A"], n + 2)
                    place_v("A")
                    act.wait_ge(xt_in, 16 * n + 32)
                    act.copy(xt16[:, 0, :], xt[:]).then_inc(xt_hi, 1)
                if b:
                    act.wait_ge(x_turned["B"], m + 1)
                    act.copy(x2t16[:, 0, :], t_bank[1][:, :]).then_inc(x_hi["B"], 1)
                if b:
                    silu(m, 0)
                    silu(m, 1)
                    load_table(ACT.Exp, 2)
                    act.wait_ge(logit_ready, m + 1)
                    act.activation(small[0][:], small[1][:], ACT.Exp).then_inc(exp_ready, 1)
                    act.activation(col[0][:].unsqueeze(2), logit[:, :, E:E + 1], ACT.Exp, scale=-1.0)\
                       .then_inc(exp_ready, 1)
                    load_table(ACT.Silu, 3)

            def weight_hi(first, last):
                act.activation(w16[:, 0, first:last, :], w[:, first:last, :], ACT.Copy, scale=W_SCALE)\
                   .then_inc(w_hi_ready, 1)

            act.wait_ge(first_in, 48)
            weight_hi(W_QA, W_QB)
            act.copy(xt16[:, 0, :], xt[:]).then_inc(xt_hi, 1)
            act.wait_ge(q_written["A"], 1)
            hi_part("q")
            act.wait_ge(k_written["A"], 1)
            hi_part("k")
            act.wait_ge(zeroed["A"], ZERO_FILLS)
            act.wait_ge(v_written["A"], 1)
            place_v("A")
            act.wait_ge(loaded, 16 * N_LOADS)
            weight_hi(W_QB, W_1)
            act.wait_ge(xt_in, 16)
            act.copy(xt16[:, 0, :], xt[:]).then_inc(xt_hi, 1)
            act.wait_ge(experts_in, 32)
            weight_hi(W_1, NW16)
            act.activation(rw16[:, 0, :], rw[:], ACT.Copy, scale=W_SCALE).then_inc(w_hi_ready, 1)
            act.wait_ge(max_turned["A"], 1)
            maxima("A")
            steps(step, act)

        @block.vector
        def _(dve):
            def lo_part(part):
                buf = split[part + "A"]
                dve.scalar_tensor_tensor(out=buf[:, 1, :], in0=side_bank[:, :], scalar=1 / W_SCALE,
                                         in1=buf[:, 0, :], op0=ALU.mult, op1=ALU.subtract)\
                   .then_inc(split_ready["A"], 1)

            def rotate(s, col_b):
                dve.scalar_tensor_tensor(
                    out=roped[:, s, :].rearrange("p (b s) -> p b s", s=S),
                    in0=side_bank[:, :].rearrange("p (b s) -> p b s", s=S),
                    scalar=bias_s[:, col_b:col_b + 1],
                    in1=rows3[:, 1:2, S * s:S * s + S].to_broadcast([P, G // S, S]),
                    op0=ALU.add, op1=ALU.mult).then_inc(roped_ready, 1)

            def maxima(n, a, t):
                for half in range(2):
                    dve.wait_ge(scores_written[a], 8 * n + 2 * t + half + 1)
                    dve.tensor_reduce(
                        neg_max[a][:, t, :].rearrange("p (r g) -> p g r", r=4)[:, 2 * half:2 * half + 2, :],
                        score_bank[half][:, :].rearrange("p (g r k) -> p g r k", g=2, k=S),
                        AX_X, ALU.max, negate=True).then_inc(max_ready[a], 1)

            def inverse_sums(n, a):
                dve.wait_ge(probs_used[a], 4 * n + 4)
                dve.reciprocal(inv_den[:], den_bank[:, 0:P]).then_inc(inv_step[a], 1)
                dve.wait_ge(inv_step[a], 2 * n + 1)
                dve.tensor_tensor(inv_own[:], inv_den[:], own_head[:], ALU.mult).then_inc(inv_step[a], 1)
                dve.wait_ge(inv_step[a], 2 * n + 2)
                dve.tensor_copy(inv_hi[:], inv_own[:]).then_inc(inv_ready[a], 1)
                dve.wait_ge(inv_ready[a], 2 * n + 1)
                dve.tensor_tensor(inv_lo[:], inv_own[:], inv_hi[:], ALU.subtract).then_inc(inv_ready[a], 1)

            def normalise(n, a, u):
                tiles = slice(2 * u, 2 * u + 2)
                dve.wait_ge(ctx_kept[a], 2 * n + u + 1)
                dve.wait_ge(spread_written[a], 2 * n + u + 1)
                dve.tensor_tensor(ctx_n[:, tiles].rearrange("p t i r q -> p (t i r q)"), y_bank[:, :],
                                  ctx_raw[a][:, tiles, :].rearrange("p t c -> p (t c)"),
                                  ALU.mult).then_inc(ctx_n_ready[a], 1)
                dve.wait_ge(ctx_n_ready[a], 2 * n + u + 1)
                dve.tensor_tensor(ctx_s[:, tiles], ctx_n[:, tiles, :, 0, :], ctx_n[:, tiles, :, 1, :],
                                  ALU.add).then_inc(ctx_s_ready[a], 1)

            def statistics(n, j, source):
                for t in range(TILES):
                    dve.bn_stats(stats[:, t, :], source[:, t, :]).then_inc(stats_ready[j], 1)
                dve.wait_ge(stats_ready[j], 4 * n + 4)
                if not isinstance(n, int):
                    dve.sem_inc(carried, 1)
                for t in range(TILES):
                    dve.bn_aggr(mean_var[:, t, :], stats[:, t, :]).then_inc(var_ready[j], 1)

            def normed_rows(n, j, source, dst):
                dve.wait_ge(rstd_ready[j], n + 1)
                for t in range(TILES):
                    ins = dve.tensor_scalar(dst[:, t, :], source[:, t, :], mean_var[:, t, 0:1],
                                            rstd[:, t:t + 1], ALU.subtract, ALU.mult)
                ins.then_inc(normed[j], 1)

            def add_residual(n, j, residual):
                dve.wait_ge(y_written[j], n + 1)
                dve.tensor_tensor(res[:].rearrange("p t d -> p (t d)"), y_bank[:, :],
                                  residual[:].rearrange("p t d -> p (t d)"), ALU.add)\
                   .then_inc(res_ready[j], 1)
                dve.wait_ge(res_ready[j], n + 1)
                statistics(n, j, res)

            def bc(a):
                return a.to_broadcast([P, TILES, E])

            done = [0]

            def chain(n, ins):
                done[0] += 1
                ins.then_inc(router_step, 1)
                dve.wait_ge(router_step, ROUTER * n + done[0])

            def router_logits(n):
                done[0] = 0
                dve.wait_ge(logits_written, n + 1)
                chain(n, dve.tensor_scalar(logit[:].rearrange("p t e -> p (t e)"),
                                           den_bank[:, 0:TILES * (E + 1)], 1 / W_SCALE, None, ALU.mult))
                if not isinstance(n, int):
                    dve.sem_inc(carried, 1)
                for t in range(TILES):
                    last = dve.max(top[:, t, :], logit[:, t, 0:E])
                chain(n, last)
                lg, first = logit[:, :, 0:E], top[:, :, 0:1]
                dve.tensor_tensor(small[1][:], lg, bc(first), ALU.subtract).then_inc(logit_ready, 1)

            def router_gates(n):
                lg, first, second = logit[:, :, 0:E], top[:, :, 0:1], top[:, :, 1:2]
                chain(n, dve.tensor_tensor(small[2][:], lg, bc(second), ALU.is_gt))
                chain(n, dve.tensor_tensor(small[3][:], lg, bc(second), ALU.is_equal))
                chain(n, dve.tensor_tensor_scan(small[4][:].rearrange("p t e -> p (t e)"),
                                                seg[:].rearrange("p t e -> p (t e)"),
                                                small[3][:].rearrange("p t e -> p (t e)"), 0.0,
                                                ALU.mult, ALU.add))
                chain(n, dve.tensor_tensor(col[1][:].unsqueeze(2), first, second, ALU.is_gt))
                chain(n, dve.tensor_scalar(col[1][:], col[1][:], -1.0, 2.0, ALU.mult, ALU.add))
                chain(n, dve.tensor_tensor(small[4][:], small[4][:], bc(col[1][:].unsqueeze(2)), ALU.is_le))
                chain(n, dve.tensor_tensor(small[4][:], small[4][:], small[3][:], ALU.mult))
                chain(n, dve.tensor_tensor(small[4][:], small[4][:], small[2][:], ALU.add))
                dve.wait_ge(exp_ready, 2 * n + 2)
                chain(n, dve.tensor_reduce(col[2][:], small[0][:], AX_X, ALU.add))
                chain(n, dve.reciprocal(col[2][:], col[2][:]))
                chain(n, dve.tensor_tensor(small[4][:], small[4][:], small[0][:], ALU.mult))
                chain(n, dve.tensor_tensor(gate[:, :, 0:E], small[4][:], bc(col[2][:].unsqueeze(2)), ALU.mult))
                chain(n, dve.tensor_scalar(col[3][:], col[0][:], 1.0, None, ALU.add))
                chain(n, dve.reciprocal(gate[:, :, E:E + 1], col[3][:].unsqueeze(2)))
                assert done[0] == ROUTER

            def shared_hidden(n):
                dve.wait_ge(silu_ready, (E + 1) * n + SHARED + 1)
                dve.wait_ge(up_written, n + 1)
                dve.scalar_tensor_tensor(out=sh_h[:], in0=t_bank[1][:, :], scalar=1 / W_SCALE,
                                         in1=act_h[:, SHARED % 2, :], op0=ALU.mult, op1=ALU.mult)\
                   .then_inc(sh_ready, 1)

            def add_expert(n, e):
                if not isinstance(n, int) or n > 0 or e > 0:
                    dve.wait_ge(expert_added, (E + 1) * n + e)
                dve.wait_ge(expert_written, (E + 1) * n + e + 1)
                before = x2 if e == 0 else moe_sum
                after = moe_sum if e < E else moe_total
                if e == E and (not isinstance(n, int) or n > 0):
                    dve.wait_ge(normed["C"], n)
                column = E if e == SHARED else min(e, E - 1)
                for t in range(TILES):
                    ins = dve.scalar_tensor_tensor(
                        out=after[:, t, :], in0=expert_bank[bank_of(e)][:, t * P:(t + 1) * P],
                        scalar=gate[:, t, column:column + 1], in1=before[:, t, :], op0=ALU.mult, op1=ALU.add)
                ins.then_inc(expert_added, 1)

            def step(n, a, b, c, d, nxt):
                m, k = n - 1, n - 2
                if b:
                    maxima(m, "B", 0)
                if c:
                    add_expert(k, 0)
                if nxt:
                    dve.wait_ge(hi_ready["A"], 2 * n + 3)
                    lo_part("q")
                if c:
                    add_expert(k, 1)
                if b:
                    maxima(m, "B", 1)
                if c:
                    add_expert(k, 2)
                if nxt:
                    dve.wait_ge(hi_ready["A"], 2 * n + 4)
                    lo_part("k")
                if b:
                    maxima(m, "B", 2)
                if c:
                    add_expert(k, 3)
                if b:
                    maxima(m, "B", 3)
                if c:
                    add_expert(k, 4)
                    add_expert(k, 5)
                if d:
                    dve.wait_ge(expert_added, (E + 1) * (n - 3) + E + 1)
                    statistics(n - 3, "C", moe_total)
                if a:
                    dve.wait_ge(k_written["B"], 2 * n + 1)
                    rotate(0, 2)
                if d:
                    dve.wait_ge(stored, 16 * (n - 3) + 16)
                    normed_rows(n - 3, "C", moe_total, x3)
                if a:
                    inverse_sums(n, "A")
                    dve.wait_ge(k_written["B"], 2 * n + 2)
                    rotate(1, 3)
                    normalise(n, "A", 0)
                    normalise(n, "A", 1)
                if nxt:
                    maxima(n + 1, "A", 0)
                    maxima(n + 1, "A", 1)
                    maxima(n + 1, "A", 2)
                if a:
                    dve.wait_ge(xn_in, 16 * n + 16)
                    add_residual(n, "A", xn)
                if b:
                    inverse_sums(m, "B")
                if a:
                    normed_rows(n, "A", res, x1)
                if b:
                    normalise(m, "B", 0)
                if a:
                    turned_lo(n, "A", den_bank, x1t16)
                if a:
                    dve.wait_ge(rope_sum_ready, 2 * n + 1)
                    dve.wait_ge(q_written["B"], 2 * n + 1)
                    rotate(0, 0)
                if b:
                    normalise(m, "B", 1)
                if a:
                    dve.wait_ge(q_written["B"], 2 * n + 2)
                    rotate(1, 1)
                if c:
                    shared_hidden(k)
                if b:
                    dve.wait_ge(biased, m + 1)
                    add_residual(m, "B", x1b)
                if c:
                    add_expert(k, 6)
                if b:
                    normed_rows(m, "B", res, x2)
                if c:
                    add_expert(k, 7)
                if b:
                    turned_lo(m, "B", t_bank[1], x2t16)
                    router_logits(m)
                if c:
                    add_expert(k, 8)
                if nxt:
                    maxima(n + 1, "A", 3)
                if b:
                    router_gates(m)

            def weight_lo(first, last):
                dve.scalar_tensor_tensor(out=w16[:, 1, first:last, :], in0=w[:, first:last, :], scalar=W_SCALE,
                                         in1=w16[:, 0, first:last, :], op0=ALU.mult, op1=ALU.subtract)\
                   .then_inc(w_split, 1)

            def turned_lo(n, a, source, dst):
                dve.wait_ge(x_hi[a], n + 1)
                dve.tensor_tensor(dst[:, 1, :], source[:, :], dst[:, 0, :], ALU.subtract)\
                   .then_inc(xt_ready[a], 1)

            def fill_q_rows(a):
                dve.memset(q_rows[a][96:128], 0.0).then_inc(zeroed[a], 1)

            def fill_k_rows(a):
                dve.memset(k_rows[a][96:128], 1.0).then_inc(zeroed[a], 1)

            dve.memset(k_block["A"][:], 0.0).then_inc(zeroed["A"], 1)
            dve.wait_ge(w_hi_ready, 1)
            weight_lo(W_QA, W_QB)
            dve.wait_ge(xt_hi, 1)
            dve.tensor_tensor(xt16[:, 1, :], xt[:], xt16[:, 0, :], ALU.subtract).then_inc(xt_split, 1)
            fill_q_rows("A")
            dve.wait_ge(hi_ready["A"], 1)
            lo_part("q")
            fill_k_rows("A")
            dve.wait_ge(hi_ready["A"], 2)
            lo_part("k")
            dve.memset(k_block["B"][:], 0.0).then_inc(zeroed["B"], 1)
            fill_q_rows("B")
            fill_k_rows("B")
            dve.wait_ge(loaded, 16 * N_LOADS)
            dve.tensor_scalar(bias_s[:], bias[:], W_SCALE, None, ALU.mult).then_inc(bias_scaled, 1)
            dve.wait_ge(w_hi_ready, 2)
            weight_lo(W_QB, W_1)
            dve.wait_ge(pool_const, 4)
            for t in range(TILES):
                maxima(0, "A", t)
            dve.wait_ge(w_hi_ready, 4)
            weight_lo(W_1, NW16)
            dve.scalar_tensor_tensor(out=rw16[:, 1, :], in0=rw[:], scalar=W_SCALE, in1=rw16[:, 0, :],
                                     op0=ALU.mult, op1=ALU.subtract).then_inc(w_split, 1)
            dve.wait_ge(v_bias_projected, 1)
            dve.tensor_tensor(out_bias[:, 0, :], y_bank[:, 0:D], rows3[:, 0, :], ALU.add)\
               .then_inc(out_bias_ready, 1)
            dve.wait_ge(bias_scaled, 1)
            steps(step, dve)


def constants():
    half = DH // 2
    freq = 1.0 / 10000.0 ** (np.arange(half, dtype=np.float32) / half)
    angle = np.arange(S, dtype=np.float32)[None, :] * np.float32(freq)[:, None]
    cos, sin = np.cos(angle).astype(np.float32), np.sin(angle).astype(np.float32)
    rope = np.concatenate([np.tile(np.concatenate([cos, cos]), (H, 1)),
                           np.tile(np.concatenate([-sin, sin]), (H, 1))], axis=1)
    rope = rope / np.float32(W_SCALE)
    masks = np.zeros((P, 4, S), np.float32)
    masks[:S, 0] = masks[:S, 1] = np.eye(S)
    masks[:S, 2] = np.where(np.arange(S)[None, :] > np.arange(S)[:, None], MASKED, 0.0)
    masks[:S, 3] = np.where(np.arange(S)[:, None] > np.arange(S)[None, :], MASKED, 0.0)
    den_ones = np.zeros((P, TILES, 2, 2, TILES, 2, 2), np.float32)
    spread = np.zeros((4, 2, 16, TILES, 2, 4, 2, 2, DH), np.float16)
    own_head = np.zeros((4, 2, 16, 2, S), np.float32)
    for x in range(2):
        own_head[:, x, :, x] = INV_SCALE
    for t in range(TILES):
        for i in range(2):
            for b in range(2):
                den_ones[64 * b:64 * b + 64, t, i, :, t, b, i] = 1.0
                for c in range(4):
                    for x in range(2):
                        spread[c, x, 4 * t + 2 * b + i, t, i, c, b, x] = 1.0 / INV_SCALE
    return dict(rope=rope, c_ident=np.eye(P, dtype=np.float32),
                c_masks=masks.astype(mybir.dt.np(BF16)), c_den_ones=den_ones.reshape(P, 8, 32),
                c_spread=spread.reshape(P, 8, P), c_own_head=own_head.reshape(P, P))


def kernel(**inputs):
    import concourse.bacc as bacc
    from concourse.bass_utils import run_bass_kernel_spmd

    a = {k: np.ascontiguousarray(v) for k, v in inputs.items()}
    x = a["x"].reshape(NG, TILES, P, D)
    group_t = lambda v: np.ascontiguousarray(v.reshape(NG, G, D).transpose(0, 2, 1))

    def swap_halves(m):
        return m.reshape(H, 2, DH // 2, -1)[:, ::-1].reshape(D, -1)

    def out_slices(m):
        rows = m.T.reshape(2, 4, 2, DH, D)
        slots = np.zeros((2, 2, 4, 2, 2, DH, D), m.dtype)
        for b in range(2):
            slots[:, b, :, b] = rows
        return slots.reshape(4, P, D)

    q_w, k_w, v_w = a["L0_xattn_q_w"], a["L0_xattn_k_w"], a["L0_xattn_v_w"]
    gate_up = a["L0_ffn_shared_gate_up"]
    slots = [a["L0_attn_w_qkv"][i * D:(i + 1) * D].T for i in range(3)]
    slots += [q_w.T, swap_halves(q_w).T, k_w.T, swap_halves(k_w).T, v_w.T]
    w_1, w_2 = a["L0_ffn_w1"], a["L0_ffn_w2"]
    slots += [*w_1[:SHARED], gate_up[:, :D], w_1[SHARED], gate_up[:, D:]]
    slots += [*w_2[:SHARED], a["L0_ffn_shared_down"], w_2[SHARED]]
    slots += [*out_slices(a["L0_attn_w_out"]), *out_slices(a["L0_xattn_o_w"])]
    consts = constants()
    q_b, k_b = a["L0_xattn_q_b"].reshape(D, 1), a["L0_xattn_k_b"].reshape(D, 1)
    row_consts = np.stack([np.broadcast_to(a["L0_xattn_o_b"], (P, D)), consts.pop("rope")], axis=1)
    v_b = np.zeros((4, 2, 2, DH, 2, P), np.float32)
    v_b[:, 0] = a["L0_xattn_v_b"].reshape(2, 4, 2, DH).transpose(1, 2, 3, 0)[..., None]
    arrays = dict(
        x=np.ascontiguousarray(x.transpose(0, 2, 1, 3)),
        x_t=np.concatenate([group_t(a["x"]), group_t(a["x"])[:1]]), ctx_t=group_t(a["ctx_1024"]),
        weights=np.ascontiguousarray(np.stack(slots, axis=1)),
        router=np.concatenate([a["L0_ffn_router_w"], a["L0_ffn_shared_gate_w"]], axis=1),
        row_consts=row_consts, v_biases=v_b.reshape(P, 2, P),
        biases=np.concatenate([q_b, swap_halves(q_b), k_b, swap_halves(k_b)], axis=1), **consts)

    nc = bacc.Bacc("TRN2", target_bir_lowering=False, num_devices=1)
    aps = {k: nc.dram_tensor("in_" + k, v.shape, mybir.dt.from_np(v.dtype), kind="ExternalInput").ap()
           for k, v in arrays.items()}
    out = nc.dram_tensor("out", (NG, P, TILES, D), F32, kind="ExternalOutput").ap()
    decoder_layer(nc, out=out, **aps)
    result = run_bass_kernel_spmd(nc, [{"in_" + k: v for k, v in arrays.items()}], core_ids=[0])
    got = result.results[0]["out"]
    return np.ascontiguousarray(got.transpose(0, 2, 1, 3)).reshape(S, S, D)
```
